# Optimizing a Trainium2 kernel written in Bass

```python
import numpy as np
import jax
import jax.numpy as jnp

def _softmax(x, axis=-1):
    return jax.nn.softmax(x, axis=axis)

def _gelu(x):
    return jax.nn.gelu(x, approximate=True)

def _silu(x):
    return jax.nn.silu(x)

def _sigmoid(x):
    return jax.nn.sigmoid(x)

def _layernorm(x, axis=-1, eps=1e-05):
    m = jnp.mean(x, axis=axis, keepdims=True)
    v = jnp.var(x, axis=axis, keepdims=True)
    return (x - m) / jnp.sqrt(v + eps)

def _scatter_add(tgt, idx, src, axis=0):
    return tgt.at[idx].add(src)

def _segment_sum(src, seg, n):
    return jax.ops.segment_sum(src, seg, n)
kernel_name = 'mk_sandwich_d1_jaxref_r8_ff4196'

def setup_inputs(seed: int=0):
    np.random.seed(seed)
    _w = jnp.asarray

    def _L0_attn_setup():
        import jax, jax.numpy as jnp
        import numpy as np
        D_MODEL = 128
        N_HEADS = 16
        HEAD_DIM = D_MODEL // N_HEADS
        D_LATENT = 32
        LAMBDA_DECAY = 0.01
        TIME_STEP = 0.01
        CLAMP = 10000.0

        def _reference_tuple_inner(x, Wq, Wk, Wv, Wo, W_down_kv, W_up_k, W_up_v):
            B, S, _ = x.shape
            q = x @ Wq
            k = x @ Wk
            v = x @ Wv
            latent_kv = (k + v) @ W_down_kv
            k_rec = latent_kv @ W_up_k
            v_rec = latent_kv @ W_up_v

            def heads(t):
                return t.reshape(B, S, N_HEADS, HEAD_DIM).transpose(0, 2, 1, 3)
            qh, kh, vh = (heads(q), heads(k_rec), heads(v_rec))
            scale = 1.0 / (jnp.sqrt(jnp.float32(D_MODEL)) + 1e-08)
            scores = jnp.einsum('bhqd,bhkd->bhqk', qh, kh) * scale
            scores = jnp.clip(jnp.nan_to_num(scores, nan=-1000000000.0), -CLAMP, CLAMP)
            idx = jnp.arange(S, dtype=jnp.float32)
            decay = jnp.exp(-LAMBDA_DECAY * TIME_STEP * jnp.abs(idx[:, None] - idx[None, :]))
            scores = scores * decay[None, None, :, :]
            scores = jnp.clip(jnp.nan_to_num(scores, nan=-1000000000.0), -CLAMP, CLAMP)
            attn = jax.nn.softmax(scores, axis=-1)
            out = jnp.einsum('bhqk,bhkd->bhqd', attn, vh)
            out = out.transpose(0, 2, 1, 3).reshape(B, S, D_MODEL)
            return (out @ Wo, latent_kv)
        key = jax.random.key(seed)
        ks = jax.random.split(key, 8)
        B, S = (2, 256)

        def w(k, i, o):
            return jax.random.normal(k, (i, o), dtype=jnp.float32) * 0.02
        return {'x': jax.random.normal(ks[0], (B, S, D_MODEL), dtype=jnp.float32), 'Wq': w(ks[1], D_MODEL, D_MODEL), 'Wk': w(ks[2], D_MODEL, D_MODEL), 'Wv': w(ks[3], D_MODEL, D_MODEL), 'Wo': w(ks[4], D_MODEL, D_MODEL), 'W_down_kv': w(ks[5], D_MODEL, D_LATENT), 'W_up_k': w(ks[6], D_LATENT, D_MODEL), 'W_up_v': w(ks[7], D_LATENT, D_MODEL)}
    _L0_attn_in = _L0_attn_setup()

    def _L0_ffn_setup():
        import jax, jax.numpy as jnp
        import numpy as np
        EMBED = 128
        HEADS = 16
        HEAD_DIM = EMBED // HEADS
        NUM_EXPERTS = 8
        TOP_K = 2
        HIDDEN = (int(2 * (4 * EMBED) / 3) + 63) // 64 * 64
        SEQ = 256
        BATCH = 2
        ROPE_BASE = 10000.0
        EPS = 1e-06

        def _rope_tables(seq_len, dim):
            inv_freq = 1.0 / ROPE_BASE ** (np.arange(0, dim, 2, dtype=np.float32) / dim)
            t = np.arange(seq_len, dtype=np.float32)
            freqs = np.einsum('i,j->ij', t, inv_freq)
            emb = np.concatenate([freqs, freqs], axis=-1)
            return (jnp.asarray(np.cos(emb)), jnp.asarray(np.sin(emb)))

        def _rotate_half(x):
            x1, x2 = jnp.split(x, 2, axis=-1)
            return jnp.concatenate([-x2, x1], axis=-1)

        def _rmsnorm(x, w):
            return x * jax.lax.rsqrt(jnp.mean(x * x, axis=-1, keepdims=True) + EPS) * w

        def _attention(x, wq, wk, wv, wo):
            B, S, _ = x.shape
            q = (x @ wq).reshape(B, S, HEADS, HEAD_DIM).transpose(0, 2, 1, 3)
            k = (x @ wk).reshape(B, S, HEADS, HEAD_DIM).transpose(0, 2, 1, 3)
            v = (x @ wv).reshape(B, S, HEADS, HEAD_DIM).transpose(0, 2, 1, 3)
            cos, sin = _rope_tables(S, HEAD_DIM)
            cos = cos[None, None]
            sin = sin[None, None]
            q = q * cos + _rotate_half(q) * sin
            k = k * cos + _rotate_half(k) * sin
            scale = HEAD_DIM ** (-0.5)
            scores = jnp.einsum('bhqd,bhkd->bhqk', q, k) * scale
            causal = jnp.triu(jnp.ones((S, S), bool), k=1)
            scores = jnp.where(causal, -jnp.inf, scores)
            attn = jax.nn.softmax(scores, axis=-1)
            out = jnp.einsum('bhqk,bhkd->bhqd', attn, v)
            out = out.transpose(0, 2, 1, 3).reshape(B, S, EMBED)
            return out @ wo

        def _moe(x, w_router, wg, wu, wd):
            B, S, E = x.shape
            xf = x.reshape(-1, E)
            logits = xf @ w_router
            probs = jax.nn.softmax(logits, axis=-1)
            topw, topi = jax.lax.top_k(probs, TOP_K)
            topw = topw / jnp.sum(topw, axis=-1, keepdims=True)
            combine = jnp.sum(jax.nn.one_hot(topi, NUM_EXPERTS, dtype=xf.dtype) * topw[..., None], axis=1)
            g = jax.nn.silu(jnp.einsum('td,xdh->txh', xf, wg))
            u = jnp.einsum('td,xdh->txh', xf, wu)
            eo = jnp.einsum('txh,xhd->txd', g * u, wd)
            out = jnp.einsum('txd,tx->td', eo, combine)
            return out.reshape(B, S, E)
        key = jax.random.key(seed)
        ks = jax.random.split(key, 12)
        s = 0.02
        return {'x': jax.random.normal(ks[0], (BATCH, SEQ, EMBED), jnp.float32), 'wq': jax.random.normal(ks[1], (EMBED, EMBED), jnp.float32) * s, 'wk': jax.random.normal(ks[2], (EMBED, EMBED), jnp.float32) * s, 'wv': jax.random.normal(ks[3], (EMBED, EMBED), jnp.float32) * s, 'wo': jax.random.normal(ks[4], (EMBED, EMBED), jnp.float32) * s, 'w_router': jax.random.normal(ks[5], (EMBED, NUM_EXPERTS), jnp.float32) * s, 'wg': jax.random.normal(ks[6], (NUM_EXPERTS, EMBED, HIDDEN), jnp.float32) * s, 'wu': jax.random.normal(ks[7], (NUM_EXPERTS, EMBED, HIDDEN), jnp.float32) * s, 'wd': jax.random.normal(ks[8], (NUM_EXPERTS, HIDDEN, EMBED), jnp.float32) * s, 'g1': jnp.ones((EMBED,), jnp.float32), 'g2': jnp.ones((EMBED,), jnp.float32)}
    _L0_ffn_in = _L0_ffn_setup()
    _d = {'L0_attn_x': _L0_attn_in['x'], 'L0_attn_Wq': _L0_attn_in['Wq'], 'L0_attn_Wk': _L0_attn_in['Wk'], 'L0_attn_Wv': _L0_attn_in['Wv'], 'L0_attn_Wo': _L0_attn_in['Wo'], 'L0_attn_W_down_kv': _L0_attn_in['W_down_kv'], 'L0_attn_W_up_k': _L0_attn_in['W_up_k'], 'L0_attn_W_up_v': _L0_attn_in['W_up_v'], 'L0_ffn_wq': _L0_ffn_in['wq'], 'L0_ffn_wk': _L0_ffn_in['wk'], 'L0_ffn_wv': _L0_ffn_in['wv'], 'L0_ffn_wo': _L0_ffn_in['wo'], 'L0_ffn_w_router': _L0_ffn_in['w_router'], 'L0_ffn_wg': _L0_ffn_in['wg'], 'L0_ffn_wu': _L0_ffn_in['wu'], 'L0_ffn_wd': _L0_ffn_in['wd'], 'L0_ffn_g1': _L0_ffn_in['g1'], 'L0_ffn_g2': _L0_ffn_in['g2']}
    _x0 = _d['L0_attn_x']
    _d['L0_attn_x'] = jax.random.normal(jax.random.fold_in(jax.random.key(seed), 1), (16, 512, 128), dtype=_x0.dtype)
    del _x0
    return _d

def reference(L0_attn_x, L0_attn_Wq, L0_attn_Wk, L0_attn_Wv, L0_attn_Wo, L0_attn_W_down_kv, L0_attn_W_up_k, L0_attn_W_up_v, L0_ffn_wq, L0_ffn_wk, L0_ffn_wv, L0_ffn_wo, L0_ffn_w_router, L0_ffn_wg, L0_ffn_wu, L0_ffn_wd, L0_ffn_g1, L0_ffn_g2):

    def _L0_attn_ref(x, Wq, Wk, Wv, Wo, W_down_kv, W_up_k, W_up_v):
        import jax, jax.numpy as jnp
        import numpy as np
        D_MODEL = 128
        N_HEADS = 16
        HEAD_DIM = D_MODEL // N_HEADS
        D_LATENT = 32
        LAMBDA_DECAY = 0.01
        TIME_STEP = 0.01
        CLAMP = 10000.0

        def _reference_tuple_inner(x, Wq, Wk, Wv, Wo, W_down_kv, W_up_k, W_up_v):
            B, S, _ = x.shape
            q = x @ Wq
            k = x @ Wk
            v = x @ Wv
            latent_kv = (k + v) @ W_down_kv
            k_rec = latent_kv @ W_up_k
            v_rec = latent_kv @ W_up_v

            def heads(t):
                return t.reshape(B, S, N_HEADS, HEAD_DIM).transpose(0, 2, 1, 3)
            qh, kh, vh = (heads(q), heads(k_rec), heads(v_rec))
            scale = 1.0 / (jnp.sqrt(jnp.float32(D_MODEL)) + 1e-08)
            scores = jnp.einsum('bhqd,bhkd->bhqk', qh, kh) * scale
            scores = jnp.clip(jnp.nan_to_num(scores, nan=-1000000000.0), -CLAMP, CLAMP)
            idx = jnp.arange(S, dtype=jnp.float32)
            decay = jnp.exp(-LAMBDA_DECAY * TIME_STEP * jnp.abs(idx[:, None] - idx[None, :]))
            scores = scores * decay[None, None, :, :]
            scores = jnp.clip(jnp.nan_to_num(scores, nan=-1000000000.0), -CLAMP, CLAMP)
            attn = jax.nn.softmax(scores, axis=-1)
            out = jnp.einsum('bhqk,bhkd->bhqd', attn, vh)
            out = out.transpose(0, 2, 1, 3).reshape(B, S, D_MODEL)
            return (out @ Wo, latent_kv)
        return _reference_tuple_inner(x, Wq, Wk, Wv, Wo, W_down_kv, W_up_k, W_up_v)[0]

    def _L0_ffn_ref(x, wq, wk, wv, wo, w_router, wg, wu, wd, g1, g2):
        import jax, jax.numpy as jnp
        import numpy as np
        EMBED = 128
        HEADS = 16
        HEAD_DIM = EMBED // HEADS
        NUM_EXPERTS = 8
        TOP_K = 2
        HIDDEN = (int(2 * (4 * EMBED) / 3) + 63) // 64 * 64
        SEQ = 256
        BATCH = 2
        ROPE_BASE = 10000.0
        EPS = 1e-06

        def _rope_tables(seq_len, dim):
            inv_freq = 1.0 / ROPE_BASE ** (np.arange(0, dim, 2, dtype=np.float32) / dim)
            t = np.arange(seq_len, dtype=np.float32)
            freqs = np.einsum('i,j->ij', t, inv_freq)
            emb = np.concatenate([freqs, freqs], axis=-1)
            return (jnp.asarray(np.cos(emb)), jnp.asarray(np.sin(emb)))

        def _rotate_half(x):
            x1, x2 = jnp.split(x, 2, axis=-1)
            return jnp.concatenate([-x2, x1], axis=-1)

        def _rmsnorm(x, w):
            return x * jax.lax.rsqrt(jnp.mean(x * x, axis=-1, keepdims=True) + EPS) * w

        def _attention(x, wq, wk, wv, wo):
            B, S, _ = x.shape
            q = (x @ wq).reshape(B, S, HEADS, HEAD_DIM).transpose(0, 2, 1, 3)
            k = (x @ wk).reshape(B, S, HEADS, HEAD_DIM).transpose(0, 2, 1, 3)
            v = (x @ wv).reshape(B, S, HEADS, HEAD_DIM).transpose(0, 2, 1, 3)
            cos, sin = _rope_tables(S, HEAD_DIM)
            cos = cos[None, None]
            sin = sin[None, None]
            q = q * cos + _rotate_half(q) * sin
            k = k * cos + _rotate_half(k) * sin
            scale = HEAD_DIM ** (-0.5)
            scores = jnp.einsum('bhqd,bhkd->bhqk', q, k) * scale
            causal = jnp.triu(jnp.ones((S, S), bool), k=1)
            scores = jnp.where(causal, -jnp.inf, scores)
            attn = jax.nn.softmax(scores, axis=-1)
            out = jnp.einsum('bhqk,bhkd->bhqd', attn, v)
            out = out.transpose(0, 2, 1, 3).reshape(B, S, EMBED)
            return out @ wo

        def _moe(x, w_router, wg, wu, wd):
            B, S, E = x.shape
            xf = x.reshape(-1, E)
            logits = xf @ w_router
            probs = jax.nn.softmax(logits, axis=-1)
            topw, topi = jax.lax.top_k(probs, TOP_K)
            topw = topw / jnp.sum(topw, axis=-1, keepdims=True)
            combine = jnp.sum(jax.nn.one_hot(topi, NUM_EXPERTS, dtype=xf.dtype) * topw[..., None], axis=1)
            g = jax.nn.silu(jnp.einsum('td,xdh->txh', xf, wg))
            u = jnp.einsum('td,xdh->txh', xf, wu)
            eo = jnp.einsum('txh,xhd->txd', g * u, wd)
            out = jnp.einsum('txd,tx->td', eo, combine)
            return out.reshape(B, S, E)
        h = x + _attention(_rmsnorm(x, g1), wq, wk, wv, wo)
        y = h + _moe(_rmsnorm(h, g2), w_router, wg, wu, wd)
        return y
    x = L0_attn_x
    x = x + _layernorm(_L0_attn_ref(_layernorm(x, axis=-1), L0_attn_Wq, L0_attn_Wk, L0_attn_Wv, L0_attn_Wo, L0_attn_W_down_kv, L0_attn_W_up_k, L0_attn_W_up_v), axis=-1)
    x = x + _layernorm(_L0_ffn_ref(_layernorm(x, axis=-1), L0_ffn_wq, L0_ffn_wk, L0_ffn_wv, L0_ffn_wo, L0_ffn_w_router, L0_ffn_wg, L0_ffn_wu, L0_ffn_wd, L0_ffn_g1, L0_ffn_g2), axis=-1)
    return x

_drawn_inputs = setup_inputs


def setup_inputs(seed=0):
    import zlib

    import numpy as np

    out = dict(_drawn_inputs(seed))
    spreads = {'L0_ffn_g1': (1.0, 0.6), 'L0_ffn_g2': (1.0, 0.6)}
    factors = {'L0_attn_Wq': 8.0,
     'L0_attn_Wk': 3.222,
     'L0_attn_Wv': 3.28,
     'L0_attn_W_up_k': 8.0,
     'L0_ffn_wq': 8.0,
     'L0_ffn_wk': 8.0,
     'L0_ffn_wv': 8.0,
     'L0_ffn_wo': 8.0,
     'L0_ffn_w_router': 8.0,
     'L0_ffn_wg': 8.0,
     'L0_ffn_wu': 8.0,
     'L0_ffn_wd': 8.0}
    for name, (base, spread) in spreads.items():
        noise = np.random.default_rng([zlib.crc32(name.encode()), seed]).standard_normal(out[name].shape)
        drawn = base * np.exp(spread * noise) if base else spread * noise
        out[name] = jnp.asarray(drawn.astype(out[name].dtype))
    for name, factor in factors.items():
        out[name] = (out[name] * factor).astype(out[name].dtype)
    return out
```

```python
from contextlib import ExitStack

import numpy as np

import concourse.bass as bass
from concourse import mybir

F32 = mybir.dt.float32
BF16 = mybir.dt.bfloat16
ALU = mybir.AluOpType
ACT = mybir.ActivationFunctionType
AX = mybir.AxisListType

P = 128
BATCH, SEQ, D = 16, 512, 128
HEADS, HD = 16, 8
QT = SEQ // P
LATENT = 32
EXPERTS, HIDDEN = 8, 384
HC = HIDDEN // P
DECAY = 0.01 * 0.01
LN_EPS, RMS_EPS = 1e-5, 1e-6
NEG = -3.0e38

DECAYED, CAUSAL = 1, 2
NB = 2 * BATCH
HEADS_PER_GROUP = 4
GROUPS = HEADS // HEADS_PER_GROUP
UNITS = HEADS_PER_GROUP * QT
PROBS = 8

Q_RUNS = [(0, 3), (0, 2), (0, 1)]
K_RUNS = [(0, 1), (0, 1), (0, 1), (1, 1), (1, 1), (2, 1)]
TERM_ROWS = 6 * HD
MAX_ROW = TERM_ROWS

Q_UP, K_DOWN, Q_DOWN, K_UP = range(4)
STACKS = {DECAYED: [Q_UP, Q_DOWN, K_DOWN, K_UP], CAUSAL: [Q_UP, K_DOWN]}
SPLIT_AT = {DECAYED: [(1, 2), (1, 5), (1, 8), (1, 11)], CAUSAL: [(1, 3), (2, 0)]}
LOADS = {DECAYED: 2 * (len(Q_RUNS) + len(K_RUNS)) + 1, CAUSAL: len(Q_RUNS) + len(K_RUNS) + 1}
MAX_LOADS = {DECAYED: 6, CAUSAL: 3}
PREP_CHAIN = {DECAYED: 2, CAUSAL: 6}


def tensors_before(p, kind):
    return 4 * p if kind == DECAYED else 4 * BATCH + 2 * (p - BATCH)


def stack_loads(p, kind):
    if kind == DECAYED:
        return 16 * LOADS[DECAYED] * (p + 1)
    return 16 * (LOADS[DECAYED] * BATCH + LOADS[CAUSAL] * (p - BATCH + 1))


def max_loads(b, g, kind):
    s = GROUPS * b + g
    if kind == DECAYED:
        return 16 * MAX_LOADS[DECAYED] * (s + 1)
    n = GROUPS * BATCH
    return 16 * (MAX_LOADS[DECAYED] * n + MAX_LOADS[CAUSAL] * (s - n + 1))


def prep_chain(p, kind):
    return 2 * p if kind == DECAYED else 2 * BATCH + 6 * (p - BATCH)


def wait(eng, sem, value):
    if isinstance(value, int) and value <= 0:
        return
    eng.wait_ge(sem, value)


def wait_apart(eng, passed, sem, value):
    wait(eng, sem, value)
    if not isinstance(value, int):
        eng.sem_inc(passed, 1)


def run_stream(eng, body):
    body(-1, 1, None, None, DECAYED)
    body(0, 0, DECAYED, None, DECAYED)
    with eng.Fori(0, (BATCH - 2) // 2) as i:
        body(2 * i + 1, 1, DECAYED, DECAYED, DECAYED)
        body(2 * i + 2, 0, DECAYED, DECAYED, DECAYED)
    body(BATCH - 1, 1, DECAYED, DECAYED, CAUSAL)
    body(BATCH, 0, CAUSAL, DECAYED, CAUSAL)
    with eng.Fori(0, (BATCH - 2) // 2) as i:
        body(2 * i + BATCH + 1, 1, CAUSAL, CAUSAL, CAUSAL)
        body(2 * i + BATCH + 2, 0, CAUSAL, CAUSAL, CAUSAL)
    body(NB - 1, 1, CAUSAL, CAUSAL, None)
    body(NB, 0, None, CAUSAL, None)


def finishing(b, g, par, ka, kp):
    if g < 2:
        return (b - 1, g + 2, 1 - par, kp) if kp else None
    return (b, g - 2, par, ka) if ka else None


def flushed(b, g, par, ka, kp):
    if g < 3:
        return (b - 1, g + 1, 1 - par, kp) if kp else None
    return (b, 0, par, ka) if ka else None


def scored(b, g, par, ka, kp):
    if g == 0:
        return (b - 1, GROUPS - 1, 1 - par, kp) if kp else None
    return (b, g - 1, par, ka) if ka else None


def attention_program(nc, t):
    ctx = ExitStack()
    with ctx:
        def sb(name, shape, dt=F32):
            return ctx.enter_context(nc.sbuf_tensor(name, shape, dt))

        def pb(name, shape, dt=F32):
            return ctx.enter_context(nc.psum_tensor(name, shape, dt))

        def sem(name):
            return ctx.enter_context(nc.semaphore(name))

        stack = [sb(f"stack{i}", [P, 4, HEADS, SEQ], BF16) for i in range(2)]
        probs = sb("probs", [P, PROBS, SEQ + P])
        scaled = sb("scaled", [P, 4, SEQ])
        parts = sb("parts", [P, 4, 3, SEQ], BF16)
        values = [sb(f"values{i}", [P, QT, HEADS, HD + 1]) for i in range(2)]
        decay = sb("decay", [P, 2 * SEQ - P])
        grow = sb("grow", [P, SEQ])
        shrink = sb("shrink", [P, SEQ])
        causal = sb("causal", [P, SEQ])
        ident = sb("ident", [P, P])
        ident_bf = sb("ident_bf", [P, P], BF16)
        ones3 = sb("ones3", [3, SEQ], BF16)
        zeros3 = sb("zeros3", [3, SEQ], BF16)
        minus_half = sb("minus_half", [P, QT])
        x_in = sb("x_in", [P, QT, D])
        xn = sb("xn", [P, QT, D])
        xr = sb("xr", [P, QT, D])
        x_t = sb("x_t", [P, SEQ])
        y = sb("y", [P, QT, D])
        residual = x_in
        heads_t = sb("heads_t", [P, SEQ])
        o = sb("o", [P, QT, HEADS, HD])
        o_t = x_t
        junk = sb("junk", [P, 2, SEQ], BF16)
        bn = sb("bn", [P, QT, 6])
        moments = sb("moments", [P, QT, 2])
        y_bn = sb("y_bn", [P, QT, 6])
        y_moments = sb("y_moments", [P, QT, 2])
        rstd = sb("rstd", [P, QT])
        rms = sb("rms", [P, QT])
        small = sb("small", [P, 4, QT])
        y_rstd = sb("y_rstd", [P, QT])
        y_small = sb("y_small", [P, QT])
        maxima = sb("maxima", [P, GROUPS, QT, HEADS_PER_GROUP])
        minus_max = sb("minus_max", [P, 2, QT, HEADS_PER_GROUP])
        max_parts = sb("max_parts", [P, QT, 3, HEADS_PER_GROUP], BF16)
        max_t = sb("max_t", [3 * HEADS_PER_GROUP, SEQ], BF16)
        inverse = sb("inverse", [P, UNITS])
        g1 = sb("g1", [P, 1])
        wq = {DECAYED: sb("wq_a", [P, D]), CAUSAL: sb("wq_f", [P, D])}
        wk = {DECAYED: sb("wk_a", [P, D]), CAUSAL: sb("wk_f", [P, D])}
        wv = {DECAYED: sb("wv_a", [P, D]), CAUSAL: sb("wv_f", [P, D])}
        wo = {DECAYED: sb("wo_a", [P, D]), CAUSAL: sb("wo_f", [P, D])}
        wq_rot = sb("wq_rot", [P, HEADS, HD])
        wk_rot = sb("wk_rot", [P, HEADS, HD])

        score_a = [pb(f"score_a{i}", [P, SEQ]) for i in range(2)]
        score_b = [pb(f"score_b{i}", [P, 2 * SEQ]) for i in range(2)]
        heads_sum = pb("heads_sum", [P, SEQ])
        bank = pb("bank", [P, SEQ])
        bank_bf = bank[:, :].bitcast(BF16)

        sp_passed, dve_passed, pool_passed = sem("sp_passed"), sem("dve_passed"), sem("pool_passed")
        consts_loaded = sem("consts_loaded")
        wkv_loaded = sem("wkv_loaded")
        dve_setup = sem("dve_setup")
        pool_setup = sem("pool_setup")
        fold_made = sem("fold_made")
        fold_taken = sem("fold_taken")
        ones_loaded = sem("ones_loaded")
        rope_loaded = sem("rope_loaded")
        x_loaded = sem("x_loaded")
        bn_done = sem("bn_done")
        moments_ready = sem("moments_ready")
        chain_done = sem("chain_done")
        xn_ready = sem("xn_ready")
        xr_ready = sem("xr_ready")
        xt_made, xt_taken = sem("xt_made"), sem("xt_taken")
        q_made, q_taken = sem("q_made"), sem("q_taken")
        k_made, k_taken = sem("k_made"), sem("k_taken")
        qrot_made, qrot_taken = sem("qrot_made"), sem("qrot_taken")
        krot_made, krot_taken = sem("krot_made"), sem("krot_taken")
        v_made, v_taken = sem("v_made"), sem("v_taken")
        scaled_ready = sem("scaled_ready")
        part0_ready = sem("part0_ready")
        rest_ready = sem("rest_ready")
        part1_ready = sem("part1_ready")
        part2_ready = sem("part2_ready")
        parts_stored = sem("parts_stored")
        stacks_loaded = sem("stacks_loaded")
        ln_stored = sem("ln_stored")
        a_scored, a_maxed = sem("a_scored"), sem("a_maxed")
        max_chain = sem("max_chain")
        maxt_made, maxt_taken = sem("maxt_made"), sem("maxt_taken")
        max_rows_loaded = sem("max_rows_loaded")
        b_scored, b_exped, b_masked = sem("b_scored"), sem("b_exped"), sem("b_masked")
        pv_done, pv_taken = sem("pv_done"), sem("pv_taken")
        ot_made, ot_taken = sem("ot_made"), sem("ot_taken")
        inverse_ready = sem("inverse_ready")
        oo_made, oo_taken = sem("oo_made"), sem("oo_taken")
        y_made, y_taken = sem("y_made"), sem("y_taken")
        y_bn_done = sem("y_bn_done")
        y_moments_ready = sem("y_moments_ready")
        y_chain = sem("y_chain")
        y_normed = sem("y_normed")
        residual_loaded = sem("residual_loaded")
        y_ready = sem("y_ready")
        y_stored = sem("y_stored")

        block = ctx.enter_context(nc.Block())

        CONSTS = [(ident, t["ident"]), (g1, t["g1"].rearrange("(d a) -> d a", a=1)),
                  (wq[DECAYED], t["Wq"]), (wo[DECAYED], t["Wo"]),
                  (wq[CAUSAL], t["wq"]), (wk[CAUSAL], t["wk"]), (wv[CAUSAL], t["wv"]),
                  (wo[CAUSAL], t["wo"]), (grow, t["grow"]), (shrink, t["shrink"]),
                  (decay, t["decay"]), (causal, t["causal"])]
        wk_in, wv_in = xr[:, 0, :], xr[:, 1, :]
        up_k, up_v = xr[0:LATENT, 2, :], xr[0:LATENT, 3, :]
        down = y[:, 0, 0:LATENT]
        wkv, wkv_t = y[:, 1, :], y[:, 2, :]
        down_t = y[0:LATENT, 3, :]

        @block.sync
        def _(sp):
            for dst, src in ((wk_in, t["Wk"]), (wv_in, t["Wv"]), (up_k, t["Up_k"]), (up_v, t["Up_v"]),
                             (down, t["Down"])):
                sp.dma_start(dst, src).then_inc(wkv_loaded, 16)
            for dst, src in CONSTS:
                sp.dma_start(dst[:, :], src).then_inc(consts_loaded, 16)
            wait_apart(sp, sp_passed, pool_setup, 2)
            wait_apart(sp, sp_passed, dve_setup, 2)
            for i in range(2):
                for k in (K_DOWN, K_UP):
                    sp.dma_start(stack[i][MAX_ROW:MAX_ROW + 3, k, :, :],
                                 ones3[:, :].unsqueeze(1).to_broadcast([3, HEADS, SEQ])).then_inc(ones_loaded, 16)
            wait_apart(sp, sp_passed, ones_loaded, 64)

            def load_max_rows(grp):
                b, g, par, kind = grp
                s = GROUPS * b + g
                wait_apart(sp, sp_passed, maxt_taken, s + 1)
                h = HEADS_PER_GROUP * g
                for q in (Q_UP, Q_DOWN)[:1 if kind == CAUSAL else 2]:
                    for i in range(3):
                        sp.dma_start(stack[par][MAX_ROW + i:MAX_ROW + i + 1, q, h:h + HEADS_PER_GROUP, :],
                                     max_t[HEADS_PER_GROUP * i:HEADS_PER_GROUP * (i + 1), :])\
                          .then_inc(max_rows_loaded, 16)

            def store_parts(p, kind, i):
                n = tensors_before(p, kind) + i
                wait_apart(sp, sp_passed, part2_ready, n + 1)
                if kind == CAUSAL or not (isinstance(p, int) and p == 0):
                    wait_apart(sp, sp_passed, stacks_loaded, stack_loads(p - 1, DECAYED if (isinstance(p, int) and p <= BATCH) else kind))
                k = STACKS[kind][i]
                for j in range(3):
                    sp.dma_start(t["scratch"][k, :, j, :, :], parts[:, i, j, :]).then_inc(parts_stored, 16)

            def load_stacks(p, kind, par):
                wait_apart(sp, sp_passed, parts_stored, 48 * (tensors_before(p, kind) + len(STACKS[kind])))
                wait_apart(sp, sp_passed, b_scored, 64 * (p - 1))
                for k in STACKS[kind]:
                    row = 0
                    for first, n in (Q_RUNS if k in (Q_UP, Q_DOWN) else K_RUNS):
                        src = t["scratch"][k, :, first:first + n, :, :].rearrange("h t d n -> (t d) h n")
                        sp.dma_start(stack[par][row:row + HD * n, k, :, :], src).then_inc(stacks_loaded, 16)
                        row += HD * n
                sp.dma_start(stack[par][MAX_ROW:MAX_ROW + 3, Q_UP, :, :],
                             zeros3[:, :].unsqueeze(1).to_broadcast([3, HEADS, SEQ])).then_inc(stacks_loaded, 16)

            def body(b, par, ka, kp, kn):
                p, q = b + 1, b - 1
                if kn:
                    wait_apart(sp, sp_passed, xn_ready, p)
                    wait_apart(sp, sp_passed, y_ready, b - 1)
                    if kn == CAUSAL:
                        wait_apart(sp, sp_passed, y_stored, 16 * (p - BATCH + 1))
                    src = t["x"][p] if kn == DECAYED else t["x1"][p - BATCH]
                    sp.dma_start(x_in[:, :, :], src.rearrange("(t p) d -> p t d", p=P)).then_inc(x_loaded, 16)
                if kn == CAUSAL and ka == DECAYED:
                    wait_apart(sp, sp_passed, k_taken, BATCH)
                    sp.dma_start(grow[:, :], t["cosines"]).then_inc(rope_loaded, 16)
                    sp.dma_start(shrink[:, :], t["sines"]).then_inc(rope_loaded, 16)
                if kp:
                    load_max_rows(scored(b, 0, par, ka, kp))
                if kn == CAUSAL:
                    wait_apart(sp, sp_passed, xn_ready, p + 1)
                    sp.dma_start(t["ln_x1"][p - BATCH].rearrange("(t p) d -> p t d", p=P), xn[:, :, :])\
                      .then_inc(ln_stored, 16)
                if ka:
                    load_max_rows(scored(b, 1, par, ka, kp))
                if kp:
                    if kn:
                        wait_apart(sp, sp_passed, xn_ready, p + 1)
                    wait_apart(sp, sp_passed, y_ready, q)
                    if kp == CAUSAL:
                        wait_apart(sp, sp_passed, ln_stored, 16 * (q - BATCH + 1))
                    src = t["x"][q] if kp == DECAYED else t["ln_x1"][q - BATCH]
                    sp.dma_start(residual[:, :, :], src.rearrange("(t p) d -> p t d", p=P))\
                      .then_inc(residual_loaded, 16)
                if kn:
                    for i in range(len(STACKS[kn])):
                        store_parts(p, kn, i)
                if ka:
                    load_max_rows(scored(b, 2, par, ka, kp))
                if kn:
                    load_stacks(p, kn, 1 - par)
                if ka:
                    load_max_rows(scored(b, 3, par, ka, kp))
                if kp:
                    wait_apart(sp, sp_passed, y_ready, q + 1)
                    dst = t["x1"][q] if kp == DECAYED else t["h"][q - BATCH]
                    sp.dma_start(dst.rearrange("(t p) d -> p t d", p=P), y[:, :, :]).then_inc(y_stored, 16)

            run_stream(sp, body)
            wait_apart(sp, sp_passed, y_stored, 16 * NB)
            wait_apart(sp, sp_passed, ln_stored, 16 * BATCH)

        @block.tensor
        def _(pe):
            pe.wait_ge(consts_loaded, 16 * len(CONSTS))
            pe.wait_ge(dve_setup, 3)
            nc.tensor.transpose(bank[:, 0:P], wkv, ident[:, :]).then_inc(fold_made, 1)
            pe.wait_ge(fold_taken, 1)
            nc.tensor.matmul(bank[0:LATENT, 0:P], down, wkv_t, start=True, stop=True).then_inc(fold_made, 1)
            pe.wait_ge(fold_taken, 2)
            nc.tensor.matmul(bank[:, 0:P], down_t, up_k, start=True, stop=True).then_inc(fold_made, 1)
            pe.wait_ge(fold_taken, 3)
            nc.tensor.matmul(bank[:, 0:P], down_t, up_v, start=True, stop=True).then_inc(fold_made, 1)
            pe.wait_ge(fold_taken, 4)
            pe.wait_ge(dve_setup, 8)
            pe.wait_ge(ones_loaded, 64)

            def score_for_max(b, par, kind, g, u):
                j, qt = divmod(u, QT)
                h, n = HEADS_PER_GROUP * g + j, 64 * b + UNITS * g + u
                wait(pe, a_maxed, n - 1)
                if g == 0 and u == 0:
                    pe.wait_ge(stacks_loaded, stack_loads(b, kind))
                keys = SEQ if kind == DECAYED else P * (qt + 1)
                nc.tensor.matmul(score_a[u % 2][:, 0:keys], stack[par][:, Q_UP, h, P * qt:P * (qt + 1)],
                                 stack[par][:, K_DOWN, h, 0:keys], start=True, stop=True).then_inc(a_scored, 1)

            def score_minus_max(grp, u):
                b, g, par, kind = grp
                kt, j = divmod(u, HEADS_PER_GROUP)
                h, n = HEADS_PER_GROUP * g + j, 64 * b + UNITS * g + u
                wait(pe, b_exped, n - 1)
                if u == 0:
                    pe.wait_ge(max_rows_loaded, max_loads(b, g, kind))
                ps, cut = score_b[u % 2], P * (kt + 1)
                keys = slice(P * kt, cut)
                if kind == DECAYED:
                    nc.tensor.matmul(ps[:, SEQ - cut:SEQ], stack[par][:, K_DOWN, h, keys],
                                     stack[par][:, Q_UP, h, 0:cut], start=True, stop=True)
                    nc.tensor.matmul(ps[:, SEQ:2 * SEQ - P * kt], stack[par][:, K_UP, h, keys],
                                     stack[par][:, Q_DOWN, h, P * kt:SEQ], start=True, stop=True)\
                      .then_inc(b_scored, 1)
                else:
                    nc.tensor.matmul(ps[:, SEQ:2 * SEQ - P * kt], stack[par][:, K_DOWN, h, keys],
                                     stack[par][:, Q_UP, h, P * kt:SEQ], start=True, stop=True)\
                      .then_inc(b_scored, 1)

            def sum_values(grp, kt):
                b, g, par, kind = grp
                pe.wait_ge(b_masked, 64 * b + UNITS * g + HEADS_PER_GROUP * (kt + 1))
                if kt == 0:
                    wait(pe, pv_taken, GROUPS * b + g)
                    pe.wait_ge(v_taken, b + 1)
                cut = P * (kt + 1)
                up = (P * kt, SEQ, cut if kind == DECAYED else 0)
                pieces = [up, (0, cut, 0)] if kind == DECAYED else [up]
                for m, (first, end, at) in enumerate(pieces):
                    for j in range(HEADS_PER_GROUP):
                        slot = (HEADS_PER_GROUP * kt + j) % PROBS
                        last = nc.tensor.matmul(
                            heads_sum[32 * j:32 * j + HD + 1, first:end],
                            values[par][:, kt, HEADS_PER_GROUP * g + j, :],
                            probs[:, slot, at:at + end - first],
                            start=(kt == 0 and m == 0), stop=(kt == QT - 1 and m == len(pieces) - 1))
                last.then_inc(pv_done, 1)

            def body(b, par, ka, kp, kn):
                p, q = b + 1, b - 1
                free = [(ot_taken, 4 * b - 3) if kp else (v_taken, b + 1) if ka else (fold_taken, 4)]

                def take_bank(taken, value):
                    wait(pe, *free[0])
                    free[0] = (taken, value)

                for g in range(GROUPS):
                    now, before = finishing(b, g, par, ka, kp), flushed(b, g, par, ka, kp)
                    maxed = scored(b, g, par, ka, kp)
                    for u in range(UNITS):
                        if u == 3 and maxed:
                            s = GROUPS * maxed[0] + maxed[1]
                            take_bank(maxt_taken, s + 1)
                            pe.wait_ge(max_chain, 5 * (s + 1))
                            for qt in range(QT):
                                last = nc.tensor.transpose(
                                    bank_bf[0:3 * HEADS_PER_GROUP, P * qt:P * (qt + 1)],
                                    max_parts[:, qt, :, :].rearrange("p a j -> p (a j)"), ident_bf[:, :])
                            last.then_inc(maxt_made, 1)
                        if u == 7 and before:
                            s = GROUPS * before[0] + before[1]
                            take_bank(ot_taken, s + 1)
                            pe.wait_ge(pv_taken, s + 1)
                            for qt in range(QT):
                                last = nc.tensor.transpose(bank[:, P * qt:P * (qt + 1)],
                                                           heads_t[:, P * qt:P * (qt + 1)], ident[:, :])
                            last.then_inc(ot_made, 1)
                        if (g, u) == (0, 9) and kn:
                            take_bank(xt_taken, p + 1)
                            if kn == DECAYED:
                                pe.wait_ge(xn_ready, p + 1)
                            else:
                                pe.wait_ge(xr_ready, p - BATCH + 1)
                            src = xn if kn == DECAYED else xr
                            for qt in range(QT):
                                last = nc.tensor.transpose(bank[:, P * qt:P * (qt + 1)], src[:, qt, :], ident[:, :])
                            last.then_inc(xt_made, 1)
                        if (g, u) == (0, 12) and kn:
                            take_bank(q_taken, p + 1)
                            pe.wait_ge(xt_taken, p + 1)
                            nc.tensor.matmul(bank[:, :], wq[kn][:, :], x_t[:, :], start=True, stop=True)\
                              .then_inc(q_made, 1)
                        if (g, u) == (0, 15) and kn == CAUSAL:
                            take_bank(qrot_taken, p - BATCH + 1)
                            nc.tensor.matmul(bank[:, :], wq_rot[:, :, :].rearrange("p h d -> p (h d)"), x_t[:, :],
                                             start=True, stop=True).then_inc(qrot_made, 1)
                        if (g, u) == ((0, 15) if kn == DECAYED else (1, 9)) and kn:
                            take_bank(k_taken, p + 1)
                            nc.tensor.matmul(bank[:, :], wk[kn][:, :], x_t[:, :], start=True, stop=True)\
                              .then_inc(k_made, 1)
                        if (g, u) == (1, 12) and kn == CAUSAL:
                            take_bank(krot_taken, p - BATCH + 1)
                            nc.tensor.matmul(bank[:, :], wk_rot[:, :, :].rearrange("p h d -> p (h d)"), x_t[:, :],
                                             start=True, stop=True).then_inc(krot_made, 1)
                        if (g, u) == (2, 9) and kn:
                            take_bank(v_taken, p + 1)
                            for kt in range(QT):
                                last = nc.tensor.matmul(bank[:, P * kt:P * (kt + 1)], x_t[:, P * kt:P * (kt + 1)],
                                                        wv[kn][:, :], start=True, stop=True)
                            last.then_inc(v_made, 1)
                        if (g, u) == (2, 12) and kp:
                            take_bank(oo_taken, q + 1)
                            pe.wait_ge(ot_taken, GROUPS * b)
                            for qt in range(QT):
                                last = nc.tensor.transpose(bank[:, P * qt:P * (qt + 1)],
                                                           o[:, qt, :, :].rearrange("p h d -> p (h d)"), ident[:, :])
                            last.then_inc(oo_made, 1)
                        if (g, u) == (2, 15) and kp:
                            take_bank(y_taken, q + 1)
                            pe.wait_ge(oo_taken, q + 1)
                            for qt in range(QT):
                                last = nc.tensor.matmul(bank[:, P * qt:P * (qt + 1)], o_t[:, P * qt:P * (qt + 1)],
                                                        wo[kp][:, :], start=True, stop=True)
                            last.then_inc(y_made, 1)
                        if ka:
                            score_for_max(b, par, ka, g, u)
                        if now:
                            score_minus_max(now, u)
                        if u == 2 and before:
                            sum_values(before, QT - 1)
                        if u in (6, 10, 14) and now:
                            sum_values(now, (u - 6) // 4)

            run_stream(pe, body)

        @block.scalar
        def _(act):
            for n, (dst, src) in enumerate(((wkv_t, bank[:, 0:P]), (down_t, bank[0:LATENT, 0:P]),
                                            (wk[DECAYED][:, :], bank[:, 0:P]), (wv[DECAYED][:, :], bank[:, 0:P]))):
                act.wait_ge(fold_made, n + 1)
                nc.scalar.activation(dst, src, ACT.Copy).then_inc(fold_taken, 1)

            def body(b, par, ka, kp, kn):
                p, q = b + 1, b - 1
                for g in range(GROUPS):
                    now, before = finishing(b, g, par, ka, kp), flushed(b, g, par, ka, kp)
                    maxed = scored(b, g, par, ka, kp)
                    for u in range(UNITS):
                        if (g, u) == (3, 0) and kp == DECAYED:
                            act.wait_ge(y_made, q + 1)
                            wait(act, y_stored, 16 * q)
                            nc.scalar.activation(y[:, :, :].rearrange("p t d -> p (t d)"), bank[:, :], ACT.Copy)\
                              .then_inc(y_taken, 1)
                        if now:
                            nb, ng, _, kind = now
                            kt = u // HEADS_PER_GROUP
                            wide = SEQ + P if kind == DECAYED else SEQ - P * kt
                            first = SEQ - P * (kt + 1) if kind == DECAYED else SEQ
                            act.wait_ge(b_scored, 64 * nb + UNITS * ng + u + 1)
                            wait(act, pv_done, 16 * nb + 4 * ng + kt - 1)
                            nc.scalar.activation(probs[:, u % PROBS, 0:wide], score_b[u % 2][:, first:first + wide],
                                                 ACT.Exp).then_inc(b_exped, 1)
                        if u == 3 and before:
                            s = GROUPS * before[0] + before[1]
                            act.wait_ge(pv_done, QT * (s + 1))
                            wait(act, ot_made, s)
                            nc.scalar.activation(heads_t[:, :], heads_sum[:, :], ACT.Copy).then_inc(pv_taken, 1)
                        if u == 4 and maxed:
                            mb, mg, _, kind = maxed
                            s = GROUPS * mb + mg
                            act.wait_ge(maxt_made, s + 1)
                            if not (isinstance(mb, int) and s == 0):
                                kb = DECAYED if isinstance(mb, int) and s <= GROUPS * BATCH else kind
                                act.wait_ge(max_rows_loaded, max_loads(mb, mg - 1, kb))
                            nc.scalar.activation(max_t[:, :], bank_bf[0:3 * HEADS_PER_GROUP, 0:SEQ], ACT.Copy)\
                              .then_inc(maxt_taken, 1)
                        if (g, u) == (0, 10) and kn:
                            act.wait_ge(xt_made, p + 1)
                            wait(act, v_made, p)
                            wait(act, y_made, b - 1)
                            if kn == DECAYED:
                                nc.scalar.activation(x_t[:, :], bank[:, :], ACT.Copy).then_inc(xt_taken, 1)
                            else:
                                nc.scalar.activation(x_t[:, :], bank[:, :], ACT.Copy, scale=g1[:, 0:1])\
                                  .then_inc(xt_taken, 1)
                        if kn:
                            for i, (sg, su) in enumerate(SPLIT_AT[kn]):
                                n = tensors_before(p, kn) + i
                                if (g, u) == (sg, su):
                                    act.wait_ge(scaled_ready, n + 1)
                                    wait(act, parts_stored, 48 * tensors_before(p, kn))
                                    nc.scalar.activation(parts[:, i, 0, :], scaled[:, i, :], ACT.Copy)\
                                      .then_inc(part0_ready, 1)
                                if (g, u) == (sg, su + 2):
                                    act.wait_ge(rest_ready, n + 1)
                                    nc.scalar.activation(parts[:, i, 1, :], scaled[:, i, :], ACT.Copy)\
                                      .then_inc(part1_ready, 1)
                        if (g, u) == (2, 10) and kn:
                            act.wait_ge(v_made, p + 1)
                            wait(act, pv_done, 16 * b)
                            act.wait_ge(dve_setup, 8)
                            nc.scalar.activation(values[1 - par][:, :, :, 0:HD],
                                                 bank[:, :].rearrange("p (t h d) -> p t h d", t=QT, h=HEADS),
                                                 ACT.Copy).then_inc(v_taken, 1)
                        if (g, u) == (2, 13) and kp:
                            act.wait_ge(oo_made, q + 1)
                            act.wait_ge(v_made, min(p + 1, NB) if isinstance(p, int) else p + 1)
                            nc.scalar.activation(o_t[:, :], bank[:, :], ACT.Copy).then_inc(oo_taken, 1)

            run_stream(act, body)

        @block.vector
        def _(dve):
            def link(n, ins):
                ins.then_inc(dve_setup, 1)
                dve.wait_ge(dve_setup, n)

            link(1, nc.vector.memset(ones3[:, :], 1.0))
            link(2, nc.vector.memset(stack[0][:, :, :, :].rearrange("p a h n -> p (a h n)").bitcast(F32), 0.0))
            dve.wait_ge(wkv_loaded, 16 * 5)
            link(3, nc.vector.tensor_tensor(wkv, wk_in, wv_in, ALU.add))
            dve.wait_ge(consts_loaded, 16 * len(CONSTS))
            link(4, nc.vector.tensor_copy(ident_bf[:, :], ident[:, :]))
            nc.vector.tensor_scalar(wq[DECAYED][:, :], wq[DECAYED][:, :],
                                    float(1.0 / (np.sqrt(np.float32(D)) + 1e-8)), None, ALU.mult)
            link(5, nc.vector.tensor_scalar(wq[CAUSAL][:, :], wq[CAUSAL][:, :], HD ** -0.5, None, ALU.mult))
            half = HD // 2
            for rot, w in ((wq_rot, wq[CAUSAL]), (wk_rot, wk[CAUSAL])):
                w3 = w[:, :].rearrange("p (h d) -> p h d", d=HD)
                nc.vector.tensor_scalar(rot[:, :, 0:half], w3[:, :, half:HD], -1.0, None, ALU.mult)
                last = nc.vector.tensor_copy(rot[:, :, half:HD], w3[:, :, 0:half])
            link(6, last)
            nc.vector.memset(heads_sum[:, :], 0.0)
            link(7, nc.vector.memset(values[0][:, :, :, :], 1.0))
            link(8, nc.vector.memset(values[1][:, :, :, :], 1.0))

            def body(b, par, ka, kp, kn):
                p, q = b + 1, b - 1
                for g in range(GROUPS):
                    before = flushed(b, g, par, ka, kp)
                    for u in range(UNITS):
                        if (g, u) == (1, 0) and kn == CAUSAL:
                            dve.wait_ge(qrot_made, p - BATCH + 1)
                            nc.vector.tensor_tensor(scaled[:, 2, :], bank[:, :], shrink[:, :], ALU.mult)\
                              .then_inc(qrot_taken, 1)
                        if (g, u) == (1, 0) and kn == DECAYED:
                            dve.wait_ge(k_made, p + 1)
                            nc.vector.tensor_tensor(scaled[:, 2, :], bank[:, :], shrink[:, :], ALU.mult)\
                              .then_inc(scaled_ready, 1)
                            nc.vector.tensor_tensor(scaled[:, 3, :], bank[:, :], grow[:, :], ALU.mult)\
                              .then_inc(scaled_ready, 1)
                            dve.wait_ge(scaled_ready, 4 * (p + 1))
                            dve.sem_inc(k_taken, 1)
                        if (g, u) == (3, 0) and kp == CAUSAL:
                            dve.wait_ge(y_made, q + 1)
                            dve.wait_ge(y_stored, 16 * q)
                            dve.wait_ge(residual_loaded, 16 * (q + 1))
                            nc.vector.tensor_tensor(y[:, :, :].rearrange("p t d -> p (t d)"), bank[:, :],
                                                    residual[:, :, :].rearrange("p t d -> p (t d)"), ALU.add)\
                              .then_inc(y_taken, 1)
                        if ka:
                            j, qt = divmod(u, QT)
                            s = GROUPS * b + g
                            if u == 0:
                                wait_apart(dve, dve_passed, max_chain, 5 * (s - 3))
                            wait_apart(dve, dve_passed, a_scored, 64 * b + UNITS * g + u + 1)
                            if ka == DECAYED:
                                table, op, keys = decay[:, SEQ - P - P * qt:2 * SEQ - P - P * qt], ALU.mult, SEQ
                            else:
                                keys = P * (qt + 1)
                                table, op = causal[:, SEQ - keys:SEQ], ALU.add
                            nc.vector.tensor_tensor_reduce(
                                out=junk[:, u % 2, 0:keys], in0=score_a[u % 2][:, 0:keys], in1=table, scale=1.0, scalar=NEG,
                                op0=op, op1=ALU.max, accum_out=maxima[:, g, qt, j:j + 1]).then_inc(a_maxed, 1)
                        if (g, u) == (0, 2) and kn:
                            dve.wait_ge(x_loaded, 16 * (p + 1))
                            for i in range(QT):
                                last = nc.vector.bn_stats(bn[:, i, :], x_in[:, i, :])
                            last.then_inc(bn_done, 1)
                            wait_apart(dve, dve_passed, bn_done, p + 1)
                            wait_apart(dve, dve_passed, chain_done, prep_chain(p, kn))
                            for i in range(QT):
                                last = nc.vector.bn_aggr(moments[:, i, :], bn[:, i, :])
                            last.then_inc(moments_ready, 1)
                        if (g, u) == (0, 5) and kn:
                            wait_apart(dve, dve_passed, chain_done, prep_chain(p, kn) + 2)
                            wait(dve, xt_made, p)
                            if kn == CAUSAL:
                                wait(dve, ln_stored, 16 * (p - BATCH))
                                wait(dve, xr_ready, p - BATCH)
                            for i in range(QT):
                                last = nc.vector.tensor_scalar(xn[:, i, :], x_in[:, i, :], moments[:, i, 0:1],
                                                               rstd[:, i:i + 1], ALU.subtract, ALU.mult)
                            last.then_inc(xn_ready, 1)
                        if u == 8 and before:
                            s = GROUPS * before[0] + before[1]
                            dve.wait_ge(ot_made, s + 1)
                            view = bank[:, :].rearrange("p (t j e) -> p t j e", t=QT, j=HEADS_PER_GROUP)
                            inv = inverse[:, :].rearrange("p (t j) -> p t j", t=QT)
                            nc.vector.reciprocal(inv, view[:, :, :, HD]).then_inc(inverse_ready, 1)
                            dve.wait_ge(inverse_ready, s + 1)
                            if before[1] == 0:
                                wait(dve, oo_made, before[0])
                            h = HEADS_PER_GROUP * before[1]
                            nc.vector.tensor_tensor(o[:, :, h:h + HEADS_PER_GROUP, :], view[:, :, :, 0:HD],
                                                    inv.unsqueeze(3).to_broadcast([P, QT, HEADS_PER_GROUP, HD]),
                                                    ALU.mult).then_inc(ot_taken, 1)
                        if (g, u) == (0, 13) and kn:
                            dve.wait_ge(q_made, p + 1)
                            wait(dve, part2_ready, tensors_before(p, kn))
                            if kn == DECAYED:
                                nc.vector.tensor_tensor(scaled[:, 0, :], bank[:, :], grow[:, :], ALU.mult)\
                                  .then_inc(scaled_ready, 1)
                                nc.vector.tensor_tensor(scaled[:, 1, :], bank[:, :], shrink[:, :], ALU.mult)\
                                  .then_inc(scaled_ready, 1)
                                dve.wait_ge(scaled_ready, 4 * p + 2)
                                dve.sem_inc(q_taken, 1)
                            else:
                                if ka == DECAYED:
                                    dve.wait_ge(rope_loaded, 32)
                                nc.vector.tensor_tensor(scaled[:, 0, :], bank[:, :], grow[:, :], ALU.mult)\
                                  .then_inc(q_taken, 1)
                        if (g, u) == (1, 10) and kn == CAUSAL:
                            dve.wait_ge(k_made, p + 1)
                            nc.vector.tensor_tensor(scaled[:, 1, :], bank[:, :], grow[:, :], ALU.mult)\
                              .then_inc(k_taken, 1)
                        if (g, u) == (1, 13) and kn == CAUSAL:
                            dve.wait_ge(krot_made, p - BATCH + 1)
                            nc.vector.tensor_tensor(scaled[:, 3, :], bank[:, :], shrink[:, :], ALU.mult)\
                              .then_inc(krot_taken, 1)
                        if kn:
                            for i, (sg, su) in enumerate(SPLIT_AT[kn]):
                                if (g, u) == (sg, su + 1):
                                    dve.wait_ge(part0_ready, tensors_before(p, kn) + i + 1)
                                    nc.vector.tensor_tensor(scaled[:, i, :], scaled[:, i, :], parts[:, i, 0, :],
                                                            ALU.subtract).then_inc(rest_ready, 1)
                        if (g, u) == (3, 2) and kp == DECAYED:
                            dve.wait_ge(y_taken, q + 1)
                            for i in range(QT):
                                last = nc.vector.bn_stats(y_bn[:, i, :], y[:, i, :])
                            last.then_inc(y_bn_done, 1)
                            wait_apart(dve, dve_passed, y_bn_done, q + 1)
                            for i in range(QT):
                                last = nc.vector.bn_aggr(y_moments[:, i, :], y_bn[:, i, :])
                            last.then_inc(y_moments_ready, 1)
                        if (g, u) == (3, 6) and kp == DECAYED:
                            dve.wait_ge(y_chain, 2 * (q + 1))
                            for i in range(QT):
                                last = nc.vector.tensor_scalar(y[:, i, :], y[:, i, :], y_moments[:, i, 0:1],
                                                               y_rstd[:, i:i + 1], ALU.subtract, ALU.mult)
                            last.then_inc(y_normed, 1)
                        if (g, u) == (3, 6) and kp == CAUSAL:
                            dve.wait_ge(y_taken, q + 1)
                            dve.sem_inc(y_ready, 1)

            run_stream(dve, body)

        @block.gpsimd
        def _(pool):
            nc.gpsimd.memset(zeros3[:, :], 0.0)
            nc.gpsimd.memset(minus_half[:, :], -0.5).then_inc(pool_setup, 1)
            nc.gpsimd.memset(stack[1][:, :, :, :].rearrange("p a h n -> p (a h n)").bitcast(F32), 0.0)\
              .then_inc(pool_setup, 1)
            wait_apart(pool, pool_passed, pool_setup, 2)

            def mask(grp, u):
                b, g, _, kind = grp
                kt, j = divmod(u, HEADS_PER_GROUP)
                wait_apart(pool, pool_passed, b_exped, 64 * b + UNITS * g + u + 1)
                tile = probs[:, u % PROBS, :]
                if kind == DECAYED:
                    low, high = tile[:, P * kt:P * (kt + 1)], tile[:, P * (kt + 1):P * (kt + 2)]
                    nc.gpsimd.affine_select(out=low, in_=low, compare_op=ALU.is_ge, fill=0.0, base=0,
                                            pattern=[[-1, P]], channel_multiplier=1)
                    nc.gpsimd.affine_select(out=high, in_=high, compare_op=ALU.is_ge, fill=0.0, base=-1,
                                            pattern=[[1, P]], channel_multiplier=-1).then_inc(b_masked, 1)
                else:
                    diag = tile[:, 0:P]
                    nc.gpsimd.affine_select(out=diag, in_=diag, compare_op=ALU.is_ge, fill=0.0, base=0,
                                            pattern=[[1, P]], channel_multiplier=-1).then_inc(b_masked, 1)

            def split_maxima(grp):
                b, g, _, _ = grp
                s = GROUPS * b + g
                m, rest, rest2 = maxima[:, g, :, :], minus_max[:, 0, :, :], minus_max[:, 1, :, :]
                part = [max_parts[:, :, i, :] for i in range(3)]
                wait_apart(pool, pool_passed, a_maxed, 64 * b + UNITS * (g + 1))
                nc.gpsimd.tensor_scalar(rest, m, -1.0, None, ALU.mult).then_inc(max_chain, 1)
                wait_apart(pool, pool_passed, max_chain, 5 * s + 1)
                wait_apart(pool, pool_passed, maxt_made, s)
                nc.gpsimd.tensor_copy(part[0], rest).then_inc(max_chain, 1)
                wait_apart(pool, pool_passed, max_chain, 5 * s + 2)
                nc.gpsimd.tensor_tensor(rest2, rest, part[0], ALU.subtract).then_inc(max_chain, 1)
                wait_apart(pool, pool_passed, max_chain, 5 * s + 3)
                nc.gpsimd.tensor_copy(part[1], rest2).then_inc(max_chain, 1)
                wait_apart(pool, pool_passed, max_chain, 5 * s + 4)
                nc.gpsimd.tensor_tensor(part[2], rest2, part[1], ALU.subtract).then_inc(max_chain, 1)

            def body(b, par, ka, kp, kn):
                p, q = b + 1, b - 1
                for g in range(GROUPS):
                    now = finishing(b, g, par, ka, kp)
                    maxed = scored(b, g, par, ka, kp)
                    if maxed:
                        split_maxima(maxed)
                    for u in range(UNITS):
                        if now:
                            mask(now, u)
                        if (g, u) == (0, 2) and kn:
                            c = prep_chain(p, kn)
                            wait_apart(pool, pool_passed, moments_ready, p + 1)
                            wait_apart(pool, pool_passed, xn_ready, p)
                            var = moments[:, :, 1]
                            nc.gpsimd.tensor_scalar(small[:, 0, :], var, LN_EPS, None, ALU.add).then_inc(chain_done, 1)
                            wait_apart(pool, pool_passed, chain_done, c + 1)
                            nc.gpsimd.tensor_tensor(rstd[:, :], small[:, 0, :], minus_half[:, :], ALU.pow)\
                              .then_inc(chain_done, 1)
                            if kn == CAUSAL:
                                wait_apart(pool, pool_passed, chain_done, c + 2)
                                nc.gpsimd.tensor_tensor(small[:, 1, :], rstd[:, :], rstd[:, :], ALU.mult)\
                                  .then_inc(chain_done, 1)
                                wait_apart(pool, pool_passed, chain_done, c + 3)
                                nc.gpsimd.tensor_tensor(small[:, 2, :], small[:, 1, :], var, ALU.mult)\
                                  .then_inc(chain_done, 1)
                                wait_apart(pool, pool_passed, chain_done, c + 4)
                                nc.gpsimd.tensor_scalar(small[:, 3, :], small[:, 2, :], RMS_EPS, None, ALU.add)\
                                  .then_inc(chain_done, 1)
                                wait_apart(pool, pool_passed, chain_done, c + 5)
                                nc.gpsimd.tensor_tensor(rms[:, :], small[:, 3, :], minus_half[:, :], ALU.pow)\
                                  .then_inc(chain_done, 1)
                        if (g, u) == (0, 6) and kn == CAUSAL:
                            wait_apart(pool, pool_passed, chain_done, prep_chain(p, kn) + 6)
                            wait_apart(pool, pool_passed, xn_ready, p + 1)
                            wait_apart(pool, pool_passed, xt_made, p)
                            nc.gpsimd.tensor_tensor(xr[:, :, :], xn[:, :, :],
                                                    rms[:, :].unsqueeze(2).to_broadcast([P, QT, D]), ALU.mult)\
                              .then_inc(xr_ready, 1)
                        if (g, u) == (1, 1) and kn == CAUSAL:
                            wait_apart(pool, pool_passed, qrot_taken, p - BATCH + 1)
                            nc.gpsimd.tensor_tensor(scaled[:, 0, :], scaled[:, 0, :], scaled[:, 2, :], ALU.add)\
                              .then_inc(scaled_ready, 1)
                        if (g, u) == (1, 14) and kn == CAUSAL:
                            wait_apart(pool, pool_passed, krot_taken, p - BATCH + 1)
                            nc.gpsimd.tensor_tensor(scaled[:, 1, :], scaled[:, 1, :], scaled[:, 3, :], ALU.add)\
                              .then_inc(scaled_ready, 1)
                        if kn:
                            for i, (sg, su) in enumerate(SPLIT_AT[kn]):
                                if (g, u) == (sg, su + 3):
                                    wait_apart(pool, pool_passed, part1_ready, tensors_before(p, kn) + i + 1)
                                    nc.gpsimd.tensor_tensor(parts[:, i, 2, :], scaled[:, i, :], parts[:, i, 1, :],
                                                            ALU.subtract).then_inc(part2_ready, 1)
                        if (g, u) == (3, 2) and kp == DECAYED:
                            wait_apart(pool, pool_passed, y_moments_ready, q + 1)
                            nc.gpsimd.tensor_scalar(y_small[:, :], y_moments[:, :, 1], LN_EPS, None, ALU.add)\
                              .then_inc(y_chain, 1)
                            wait_apart(pool, pool_passed, y_chain, 2 * q + 1)
                            nc.gpsimd.tensor_tensor(y_rstd[:, :], y_small[:, :], minus_half[:, :], ALU.pow)\
                              .then_inc(y_chain, 1)
                        if (g, u) == (3, 6) and kp == DECAYED:
                            wait_apart(pool, pool_passed, y_normed, q + 1)
                            wait_apart(pool, pool_passed, residual_loaded, 16 * (q + 1))
                            nc.gpsimd.tensor_tensor(y[:, :, :], y[:, :, :], residual[:, :, :], ALU.add)\
                              .then_inc(y_ready, 1)

            run_stream(pool, body)


def experts_program(nc, t):
    ctx = ExitStack()
    with ctx:
        def sb(name, shape, dt=F32):
            return ctx.enter_context(nc.sbuf_tensor(name, shape, dt))

        def pb(name, shape, dt=F32):
            return ctx.enter_context(nc.psum_tensor(name, shape, dt))

        def sem(name):
            return ctx.enter_context(nc.semaphore(name))

        w_gate = sb("w_gate", [P, EXPERTS, HIDDEN])
        w_up = sb("w_up", [P, EXPERTS, HIDDEN])
        w_down = sb("w_down", [P, EXPERTS, HC, D])
        router = sb("router", [P, EXPERTS])
        g2 = sb("g2", [P, 1])
        eye = sb("eye", [P, P])
        lower = sb("lower", [P, EXPERTS, EXPERTS])
        half = sb("half", [P, QT])
        h_in = [sb(f"h_in{i}", [P, QT, D]) for i in range(2)]
        hn = sb("hn", [P, QT, D])
        h_t = [sb(f"h_t{i}", [P, SEQ]) for i in range(2)]
        x1 = [sb(f"x1_{i}", [P, QT, D]) for i in range(2)]
        gated = [sb(f"gated{i}", [P, SEQ]) for i in range(2)]
        hidden = [sb(f"hidden{i}", [P, HC, SEQ]) for i in range(2)]
        acc = [sb(f"acc{i}", [P, QT, D]) for i in range(2)]
        weight = [sb(f"weight{i}", [P, QT, EXPERTS]) for i in range(2)]
        bn = sb("h_bn", [P, QT, 6])
        mom = sb("h_moments", [P, QT, 2])
        square = sb("square", [P, QT])
        rms = sb("h_rms", [P, QT])
        bn2 = sb("out_bn", [P, QT, 6])
        mom2 = sb("out_moments", [P, QT, 2])
        small2 = sb("out_small", [P, QT])
        rstd2 = sb("out_rstd", [P, QT])
        top = sb("top", [P, QT])
        e_in = sb("e_in", [P, QT, EXPERTS])
        e = sb("e", [P, QT, EXPERTS])
        greater = sb("greater", [P, QT, EXPERTS, EXPERTS])
        ties = sb("ties", [P, QT, EXPERTS, EXPERTS])
        rank = sb("rank", [P, QT, EXPERTS])
        total = sb("total", [P, QT])

        gate_ps = [pb(f"gate_ps{i}", [P, SEQ]) for i in range(2)]
        up_ps = [pb(f"up_ps{i}", [P, SEQ]) for i in range(2)]
        down_ps = [pb(f"down_ps{i}", [P, QT, D]) for i in range(2)]
        turn_ps = pb("turn_ps", [P, SEQ])
        logits = pb("logits", [P, QT, EXPERTS])

        weights_loaded = sem("weights_loaded")
        sp_passed, dve_passed, pool_passed = sem("sp_passed"), sem("dve_passed"), sem("pool_passed")
        half_ready = sem("half_ready")
        h_loaded = sem("h_loaded")
        prep_dve = sem("prep_dve")
        rms_chain = sem("rms_chain")
        total_ready = sem("total_ready")
        hn_ready = sem("hn_ready")
        ht_made, ht_taken = sem("ht_made"), sem("ht_taken")
        logits_made = sem("logits_made")
        route_a = sem("route_a")
        e_ready = sem("e_ready")
        route_b = sem("route_b")
        gate_made, gate_taken = sem("gate_made"), sem("gate_taken")
        up_made, hidden_made = sem("up_made"), sem("hidden_made")
        down_made, down_taken = sem("down_made"), sem("down_taken")
        out_dve = sem("out_dve")
        out_chain = sem("out_chain")
        out_normed = sem("out_normed")
        x1_loaded = sem("x1_loaded")
        out_ready = sem("out_ready")
        out_stored = sem("out_stored")

        block = ctx.enter_context(nc.Block())
        NW = 7
        ROUTE = 8

        def rows(tensor, n):
            return tensor[n].rearrange("(t p) d -> p t d", p=P)

        def run_groups(eng, body):
            body(-1, 1, True)
            body(0, 0, True)
            with eng.Fori(0, (BATCH - 2) // 2) as i:
                body(2 * i + 1, 1, True)
                body(2 * i + 2, 0, True)
            body(BATCH - 1, 1, False)

        @block.sync
        def _(sp):
            sp.dma_start(eye[:, :], t["ident"]).then_inc(weights_loaded, 16)
            sp.dma_start(g2[:, :], t["g2"].rearrange("(d a) -> d a", a=1)).then_inc(weights_loaded, 16)
            sp.dma_start(router[:, :], t["w_router"]).then_inc(weights_loaded, 16)
            sp.dma_start(lower[:, :, :], t["lower"]).then_inc(weights_loaded, 16)
            sp.dma_start(h_in[0][:, :, :], rows(t["h"], 0)).then_inc(h_loaded, 16)
            sp.dma_start(w_gate[:, :, :], t["wg"].rearrange("x d h -> d x h")).then_inc(weights_loaded, 16)
            sp.dma_start(w_up[:, :, :], t["wu"].rearrange("x d h -> d x h")).then_inc(weights_loaded, 16)
            sp.dma_start(w_down[:, :, :, :], t["wd"].rearrange("x (c p) d -> p x c d", p=P))\
              .then_inc(weights_loaded, 16)

            def body(n, par, more):
                real = not (isinstance(n, int) and n < 0)
                if real:
                    wait_apart(sp, sp_passed, out_ready, n - 1)
                    wait_apart(sp, sp_passed, x1_loaded, 16 * n)
                    sp.dma_start(x1[par][:, :, :], rows(t["x1"], n)).then_inc(x1_loaded, 16)
                if more and real:
                    wait_apart(sp, sp_passed, down_taken, EXPERTS * n)
                    wait_apart(sp, sp_passed, h_loaded, 16 * (n + 1))
                    sp.dma_start(h_in[1 - par][:, :, :], rows(t["h"], n + 1)).then_inc(h_loaded, 16)
                if real:
                    wait_apart(sp, sp_passed, out_ready, n + 1)
                    sp.dma_start(rows(t["out"], n), acc[par][:, :, :]).then_inc(out_stored, 16)

            run_groups(sp, body)
            wait_apart(sp, sp_passed, out_stored, 16 * BATCH)

        @block.tensor
        def _(pe):
            pe.wait_ge(weights_loaded, 16 * NW)

            def down(n, par, x):
                m = EXPERTS * n + x
                pe.wait_ge(hidden_made, HC * (m + 1))
                wait(pe, down_taken, m - 1)
                for qt in range(QT):
                    for c in range(HC):
                        last = nc.tensor.matmul(down_ps[x % 2][:, qt, :], hidden[x % 2][:, c, P * qt:P * (qt + 1)],
                                                w_down[:, x, c, :], start=(c == 0), stop=(c == HC - 1))
                last.then_inc(down_made, 1)

            def body(n, par, more):
                real = not (isinstance(n, int) and n < 0)
                for x in range(EXPERTS):
                    if x == 2 and more:
                        pe.wait_ge(hn_ready, n + 2)
                        wait(pe, ht_taken, n + 1)
                        for qt in range(QT):
                            last = nc.tensor.transpose(turn_ps[:, P * qt:P * (qt + 1)], hn[:, qt, :], eye[:, :])
                        last.then_inc(ht_made, 1)
                    if x == 4 and more:
                        pe.wait_ge(ht_taken, n + 2)
                        wait(pe, route_a, 2 * (n + 1))
                        for qt in range(QT):
                            last = nc.tensor.matmul(logits[:, qt, :], h_t[1 - par][:, P * qt:P * (qt + 1)],
                                                    router[:, :], start=True, stop=True)
                        last.then_inc(logits_made, 1)
                    if not real:
                        continue
                    if x == 0:
                        pe.wait_ge(ht_taken, n + 1)
                    for c in range(HC):
                        k = HC * (EXPERTS * n + x) + c
                        wait(pe, gate_taken, k - 1)
                        nc.tensor.matmul(gate_ps[(HC * x + c) % 2][:, :], w_gate[:, x, P * c:P * (c + 1)],
                                         h_t[par][:, :], start=True, stop=True).then_inc(gate_made, 1)
                        wait(pe, hidden_made, k - 1)
                        nc.tensor.matmul(up_ps[(HC * x + c) % 2][:, :], w_up[:, x, P * c:P * (c + 1)],
                                         h_t[par][:, :], start=True, stop=True).then_inc(up_made, 1)
                    if x > 0:
                        down(n, par, x - 1)
                if real:
                    down(n, par, EXPERTS - 1)

            run_groups(pe, body)

        @block.scalar
        def _(act):
            act.wait_ge(weights_loaded, 16 * NW)

            def body(n, par, more):
                real = not (isinstance(n, int) and n < 0)
                for x in range(EXPERTS):
                    if x == 2 and more:
                        act.wait_ge(ht_made, n + 2)
                        wait(act, down_made, EXPERTS * n)
                        nc.scalar.activation(h_t[1 - par][:, :], turn_ps[:, :], ACT.Copy, scale=g2[:, 0:1])\
                          .then_inc(ht_taken, 1)
                    if x == 5 and more:
                        act.wait_ge(route_a, 2 * (n + 2))
                        wait(act, route_b, ROUTE * (n + 1))
                        nc.scalar.activation(e[:, :, :], e_in[:, :, :], ACT.Exp).then_inc(e_ready, 1)
                    if not real:
                        continue
                    for c in range(HC):
                        k = HC * (EXPERTS * n + x) + c
                        act.wait_ge(gate_made, k + 1)
                        wait(act, hidden_made, k - 1)
                        nc.scalar.activation(gated[(HC * x + c) % 2][:, :], gate_ps[(HC * x + c) % 2][:, :], ACT.Silu)\
                          .then_inc(gate_taken, 1)

            run_groups(act, body)

        @block.vector
        def _(dve):
            dve.wait_ge(weights_loaded, 16 * NW)

            def body(n, par, more):
                real = not (isinstance(n, int) and n < 0)

                def add_up(x):
                    m = EXPERTS * n + x
                    dve.wait_ge(down_made, m + 1)
                    if x == 0:
                        dve.wait_ge(route_b, ROUTE * (n + 1))
                        wait(dve, out_stored, 16 * (n - 1))
                    else:
                        dve.wait_ge(down_taken, m)
                    for qt in range(QT):
                        last = nc.vector.scalar_tensor_tensor(
                            out=acc[par][:, qt, :], in0=down_ps[x % 2][:, qt, :], scalar=weight[par][:, qt, x:x + 1],
                            in1=(h_in if x == 0 else acc)[par][:, qt, :], op0=ALU.mult, op1=ALU.add)
                    last.then_inc(down_taken, 1)

                for x in range(EXPERTS):
                    if x == 1 and more:
                        dve.wait_ge(h_loaded, 16 * (n + 2))
                        for i in range(QT):
                            last = nc.vector.bn_stats(bn[:, i, :], h_in[1 - par][:, i, :])
                        last.then_inc(prep_dve, 1)
                        wait_apart(dve, dve_passed, prep_dve, 2 * (n + 1) + 1)
                        for i in range(QT):
                            last = nc.vector.bn_aggr(mom[:, i, :], bn[:, i, :])
                        last.then_inc(prep_dve, 1)
                    if x == 4 and more:
                        k = 2 * (n + 1)
                        dve.wait_ge(logits_made, n + 2)
                        nc.vector.reduce_max(top[:, :], logits[:, :, :], AX.X).then_inc(route_a, 1)
                        dve.wait_ge(route_a, k + 1)
                        nc.vector.tensor_tensor(e_in[:, :, :], logits[:, :, :],
                                                top[:, :].unsqueeze(2).to_broadcast([P, QT, EXPERTS]), ALU.subtract)\
                          .then_inc(route_a, 1)
                    if x == 6 and more:
                        k = ROUTE * (n + 1)
                        dve.wait_ge(e_ready, n + 2)
                        wide = [P, QT, EXPERTS, EXPERTS]
                        other, own = e[:, :, :].unsqueeze(2).to_broadcast(wide), e[:, :, :].unsqueeze(3).to_broadcast(wide)
                        nc.vector.tensor_tensor(greater[:, :, :, :], other, own, ALU.is_gt).then_inc(route_b, 1)
                        nc.vector.tensor_tensor(ties[:, :, :, :], other, own, ALU.is_equal).then_inc(route_b, 1)
                        dve.wait_ge(route_b, k + 2)
                        nc.vector.tensor_tensor(ties[:, :, :, :], ties[:, :, :, :],
                                                lower[:, :, :].unsqueeze(1).to_broadcast(wide), ALU.mult)\
                          .then_inc(route_b, 1)
                        dve.wait_ge(route_b, k + 3)
                        nc.vector.tensor_tensor(ties[:, :, :, :], ties[:, :, :, :], greater[:, :, :, :], ALU.add)\
                          .then_inc(route_b, 1)
                        dve.wait_ge(route_b, k + 4)
                        nc.vector.reduce_sum(rank[:, :, :], ties[:, :, :, :], AX.X).then_inc(route_b, 1)
                        dve.wait_ge(route_b, k + 5)
                        nc.vector.scalar_tensor_tensor(out=rank[:, :, :], in0=rank[:, :, :], scalar=1.5,
                                                       in1=e[:, :, :], op0=ALU.is_lt, op1=ALU.mult)\
                          .then_inc(route_b, 1)
                        dve.wait_ge(route_b, k + 6)
                        nc.vector.reduce_sum(total[:, :], rank[:, :, :], AX.X).then_inc(total_ready, 1)
                        dve.wait_ge(total_ready, n + 2)
                        nc.vector.reciprocal(total[:, :], total[:, :]).then_inc(route_b, 1)
                        dve.wait_ge(route_b, k + 7)
                        nc.vector.tensor_tensor(weight[1 - par][:, :, :], rank[:, :, :],
                                                total[:, :].unsqueeze(2).to_broadcast([P, QT, EXPERTS]), ALU.mult)\
                          .then_inc(route_b, 1)
                    if not real:
                        continue
                    for c in range(HC):
                        k = HC * (EXPERTS * n + x) + c
                        dve.wait_ge(up_made, k + 1)
                        dve.wait_ge(gate_taken, k + 1)
                        if c == 0:
                            wait(dve, down_made, EXPERTS * n + x - 1)
                        nc.vector.tensor_tensor(hidden[x % 2][:, c, :], up_ps[(HC * x + c) % 2][:, :],
                                                gated[(HC * x + c) % 2][:, :], ALU.mult).then_inc(hidden_made, 1)
                    if x > 0:
                        add_up(x - 1)
                if real:
                    add_up(EXPERTS - 1)
                    dve.wait_ge(down_taken, EXPERTS * (n + 1))
                    for i in range(QT):
                        last = nc.vector.bn_stats(bn2[:, i, :], acc[par][:, i, :])
                    last.then_inc(out_dve, 1)
                    wait_apart(dve, dve_passed, out_dve, 2 * n + 1)
                    for i in range(QT):
                        last = nc.vector.bn_aggr(mom2[:, i, :], bn2[:, i, :])
                    last.then_inc(out_dve, 1)
                    dve.wait_ge(out_chain, 2 * (n + 1))
                    for i in range(QT):
                        last = nc.vector.tensor_scalar(acc[par][:, i, :], acc[par][:, i, :], mom2[:, i, 0:1],
                                                       rstd2[:, i:i + 1], ALU.subtract, ALU.mult)
                    last.then_inc(out_normed, 1)

            run_groups(dve, body)

        @block.gpsimd
        def _(pool):
            nc.gpsimd.memset(half[:, :], -0.5).then_inc(half_ready, 1)
            wait_apart(pool, pool_passed, half_ready, 1)

            def body(n, par, more):
                real = not (isinstance(n, int) and n < 0)
                if more:
                    k = 4 * (n + 1)
                    wait_apart(pool, pool_passed, prep_dve, 2 * (n + 2))
                    nc.gpsimd.tensor_tensor(square[:, :], mom[:, :, 0], mom[:, :, 0], ALU.mult).then_inc(rms_chain, 1)
                    wait_apart(pool, pool_passed, rms_chain, k + 1)
                    nc.gpsimd.tensor_tensor(square[:, :], square[:, :], mom[:, :, 1], ALU.add).then_inc(rms_chain, 1)
                    wait_apart(pool, pool_passed, rms_chain, k + 2)
                    nc.gpsimd.tensor_scalar(square[:, :], square[:, :], RMS_EPS, None, ALU.add).then_inc(rms_chain, 1)
                    wait_apart(pool, pool_passed, rms_chain, k + 3)
                    nc.gpsimd.tensor_tensor(rms[:, :], square[:, :], half[:, :], ALU.pow).then_inc(rms_chain, 1)
                    wait_apart(pool, pool_passed, rms_chain, k + 4)
                    wait_apart(pool, pool_passed, ht_made, n + 1)
                    nc.gpsimd.tensor_tensor(hn[:, :, :], h_in[1 - par][:, :, :],
                                            rms[:, :].unsqueeze(2).to_broadcast([P, QT, D]), ALU.mult)\
                      .then_inc(hn_ready, 1)
                if real:
                    wait_apart(pool, pool_passed, out_dve, 2 * (n + 1))
                    nc.gpsimd.tensor_scalar(small2[:, :], mom2[:, :, 1], LN_EPS, None, ALU.add).then_inc(out_chain, 1)
                    wait_apart(pool, pool_passed, out_chain, 2 * n + 1)
                    nc.gpsimd.tensor_tensor(rstd2[:, :], small2[:, :], half[:, :], ALU.pow).then_inc(out_chain, 1)
                    wait_apart(pool, pool_passed, out_normed, n + 1)
                    wait_apart(pool, pool_passed, x1_loaded, 16 * (n + 1))
                    nc.gpsimd.tensor_tensor(acc[par][:, :, :], acc[par][:, :, :], x1[par][:, :, :], ALU.add)\
                      .then_inc(out_ready, 1)

            run_groups(pool, body)


def sandwich_kernel(nc, t):
    t["scratch"] = nc.dram_tensor("split_parts", (4, HEADS, 3, HD, SEQ), BF16, kind="Internal").ap()
    for name in ("x1", "ln_x1", "h"):
        t[name] = nc.dram_tensor(f"kept_{name}", (BATCH, SEQ, D), F32, kind="Internal").ap()
    attention_program(nc, t)
    experts_program(nc, t)


_NAMES = {"L0_attn_x": "x", "L0_attn_Wq": "Wq", "L0_attn_Wk": "Wk", "L0_attn_Wv": "Wv", "L0_attn_Wo": "Wo",
          "L0_attn_W_down_kv": "Down", "L0_attn_W_up_k": "Up_k", "L0_attn_W_up_v": "Up_v",
          "L0_ffn_wq": "wq", "L0_ffn_wk": "wk", "L0_ffn_wv": "wv", "L0_ffn_wo": "wo",
          "L0_ffn_w_router": "w_router", "L0_ffn_wg": "wg", "L0_ffn_wu": "wu", "L0_ffn_wd": "wd",
          "L0_ffn_g1": "g1", "L0_ffn_g2": "g2"}


def tables():
    i = np.arange(SEQ, dtype=np.float64)
    off = np.arange(P)[:, None] - (np.arange(2 * SEQ - P)[None, :] - (SEQ - P))
    decay = np.exp(-DECAY * np.abs(off) - DECAY * off)
    inv = 1.0 / 10000.0 ** (np.arange(0, HD, 2, dtype=np.float32) / HD)
    freqs = np.einsum("i,j->ij", np.arange(SEQ, dtype=np.float32), inv.astype(np.float32))
    emb = np.concatenate([freqs, freqs], axis=-1)
    rows = np.arange(P)
    causal = np.zeros((P, SEQ), np.float32)
    causal[:, SEQ - P:] = np.where(rows[None, :] > rows[:, None], NEG, 0.0)
    n = np.arange(EXPERTS)
    made = {
        "ident": np.eye(P), "decay": decay,
        "grow": np.broadcast_to(np.exp(DECAY * i), (P, SEQ)), "shrink": np.broadcast_to(np.exp(-DECAY * i), (P, SEQ)),
        "cosines": np.tile(np.cos(emb).T, (HEADS, 1)), "sines": np.tile(np.sin(emb).T, (HEADS, 1)),
        "causal": causal, "lower": np.broadcast_to((n[None, :] < n[:, None]), (P, EXPERTS, EXPERTS)),
    }
    return {k: np.ascontiguousarray(v, dtype=np.float32) for k, v in made.items()}


def kernel(**inputs):
    import concourse.bacc as bacc
    from concourse.bass_utils import run_bass_kernel_spmd

    nc = bacc.Bacc("TRN2", target_bir_lowering=False, num_devices=1)
    arrays, t = {}, {}
    named = {short: np.ascontiguousarray(inputs[name]) for name, short in _NAMES.items()}
    for name, a in {**named, **tables()}.items():
        arrays[f"in_{name}"] = a
        t[name] = nc.dram_tensor(f"in_{name}", a.shape, mybir.dt.from_np(a.dtype), kind="ExternalInput").ap()
    t["out"] = nc.dram_tensor("out_0", (BATCH, SEQ, D), F32, kind="ExternalOutput").ap()
    sandwich_kernel(nc, t)
    r = run_bass_kernel_spmd(nc, [arrays], core_ids=[0])
    return r.results[0]["out_0"]
```

```python
from contextlib import ExitStack

import numpy as np

import concourse.bass as bass
from concourse import mybir

F32 = mybir.dt.float32
BF16 = mybir.dt.bfloat16
F32R = mybir.dt.float32r
I32 = mybir.dt.int32
ALU = mybir.AluOpType
ACT = mybir.ActivationFunctionType
AX = mybir.AxisListType

P = 128
BATCH, SEQ, D = 16, 512, 128
HEADS, HD = 16, 8
QT = SEQ // P
LATENT = 32
EXPERTS, HIDDEN = 8, 384
HC = HIDDEN // P
DECAY = 0.01 * 0.01
CLAMP = 10000.0
SCALE = float(1.0 / (np.sqrt(np.float32(D)) + 1e-8))
LN_EPS, RMS_EPS = 1e-5, 1e-6
NEG = -3.0e38

DECAYED, CAUSAL = 1, 2
HEADS_PER_GROUP = 4
GROUPS = HEADS // HEADS_PER_GROUP
UNITS = HEADS_PER_GROUP * QT

TERMS = 6
Q_RUNS = [(0, 3, 0), (3, 5, 0), (5, 6, 0)]
K_RUNS = [(0, 3, 0), (3, 5, 1), (5, 6, 2)]
TERM_ROWS = TERMS * HD
MAX_ROW = TERM_ROWS

Q_UP, K_DOWN, Q_DOWN, K_UP = range(4)
STACKS = {DECAYED: [Q_UP, Q_DOWN, K_DOWN, K_UP], CAUSAL: [Q_UP, K_DOWN]}
SPLIT_AT = {DECAYED: [(1, 6), (1, 9), (2, 2), (2, 6)], CAUSAL: [(1, 12), (2, 7)]}
SUM_IN_SAME = {u: [u - 7] for u in range(7, UNITS)}
SUM_IN_NEXT = {0: [9], 1: [10], 2: [11], 3: [12], 4: [13], 5: [14, 15]}
MAX_TURN_AT = {DECAYED: 7, CAUSAL: 6}
TURN_AT = {DECAYED: (0, 15), CAUSAL: (1, 1)}
QUERIES_AT = {DECAYED: (1, 3), CAUSAL: (1, 4)}
NEAR_LOADS = 3
FAR_LOADS = 2
MAX_LOADS = {DECAYED: 6, CAUSAL: 3}
PREP_CHAIN = {DECAYED: 2, CAUSAL: 3}


def wait(eng, sem, value):
    if isinstance(value, int) and value <= 0:
        return
    eng.wait_ge(sem, value)


def wait_apart(eng, passed, sem, value):
    wait(eng, sem, value)
    if not isinstance(value, int):
        eng.sem_inc(passed, 1)


def finishing(b, g, par, ka, kp):
    if g < 2:
        return (b - 1, g + 2, 1 - par, kp) if kp else None
    return (b, g - 2, par, ka) if ka else None


def flushed(b, g, par, ka, kp):
    if g < 3:
        return (b - 1, g + 1, 1 - par, kp) if kp else None
    return (b, 0, par, ka) if ka else None


def scored(b, g, par, ka, kp):
    if g == 0:
        return (b - 1, GROUPS - 1, 1 - par, kp) if kp else None
    return (b, g - 1, par, ka) if ka else None


def attention_program(nc, t, decayed, sems, bounded=None):
    batches = decayed + BATCH
    again = "" if decayed else "_again"

    def tensors_before(p, kind):
        return 4 * p if kind == DECAYED else 4 * decayed + 2 * (p - decayed)

    def max_loads(b, g, kind):
        s, n = GROUPS * b + g, GROUPS * decayed
        if kind == DECAYED:
            return 16 * MAX_LOADS[DECAYED] * (s + 1)
        return 16 * (MAX_LOADS[DECAYED] * n + MAX_LOADS[CAUSAL] * (s - n + 1))

    def prep_chain(p, kind):
        return PREP_CHAIN[DECAYED] * (p if kind == DECAYED else decayed) + \
            (0 if kind == DECAYED else PREP_CHAIN[CAUSAL] * (p - decayed))

    def run_stream(eng, body):
        body(-1, 1, None, None, DECAYED if decayed else CAUSAL)
        for kind, first in ((DECAYED, 0), (CAUSAL, decayed)):
            if kind == DECAYED and not decayed:
                continue
            body(first, 0, kind, DECAYED if first else None, kind)
            if first == 0:
                body(1, 1, kind, kind, kind)
                body(2, 0, kind, kind, kind)
                first = 2
            pairs = (BATCH - 2 - first % BATCH) // 2
            with eng.Fori(0, pairs) as i:
                body(2 * i + first + 1, 1, kind, kind, kind)
                body(2 * i + first + 2, 0, kind, kind, kind)
            first += 2 * pairs + 1
            body(first, 1, kind, kind, CAUSAL if kind == DECAYED else None)
        body(batches, 0, None, CAUSAL, None)

    ctx = ExitStack()
    with ctx:
        def sb(name, shape, dt=F32):
            return ctx.enter_context(nc.sbuf_tensor(name + again, shape, dt))

        def pb(name, shape, dt=F32):
            return ctx.enter_context(nc.psum_tensor(name + again, shape, dt))

        def sem(name):
            if name not in sems:
                sems[name] = nc.alloc_semaphore(name)
            return sems[name]

        near = [sb(f"near{i}", [P, 2, HEADS, SEQ], BF16) for i in range(2)]
        far = sb("far", [P, 2, HEADS, SEQ], BF16)
        probs = sb("probs", [P, UNITS, SEQ + P])
        scaled = sb("scaled", [P, 4, SEQ])
        parts = sb("parts", [P, 4, 3, SEQ], BF16)
        values = [sb(f"values{i}", [P, QT, HEADS, HD + 1]) for i in range(2)]
        decay = sb("decay", [P, 2 * SEQ - P])
        grow = sb("grow", [P, SEQ])
        shrink = sb("shrink", [P, SEQ])
        causal = sb("causal", [P, SEQ])
        ident = sb("ident", [P, P])
        ident_bf = sb("ident_bf", [P, P], BF16)
        ones3 = sb("ones3", [3, SEQ], BF16)
        zeros3 = sb("zeros3", [3, SEQ], BF16)
        minus_half = sb("minus_half", [P, 2 * QT])
        x_in = sb("x_in", [P, QT, D])
        xn = sb("xn", [P, QT, D])
        xr = sb("xr", [P, QT, D])
        x_t = sb("x_t", [P, SEQ])
        y = sb("y", [P, QT, D])
        residual = x_in
        heads_t = sb("heads_t", [P, SEQ])
        o = sb("o", [P, QT, HEADS, HD])
        o_t = sb("o_t", [P, SEQ])
        junk = sb("junk", [P, 4, SEQ], BF16)
        bn = sb("bn", [P, QT, 6])
        moments = sb("moments", [P, QT, 2])
        y_bn = sb("y_bn", [P, QT, 6])
        y_moments = sb("y_moments", [P, QT, 2])
        rstds = sb("rstds", [P, 2, QT])
        small = sb("small", [P, 2, QT])
        y_rstd = sb("y_rstd", [P, QT])
        y_small = sb("y_small", [P, QT])
        maxima = sb("maxima", [P, GROUPS, QT, HEADS_PER_GROUP])
        minus_max = sb("minus_max", [P, 2, QT, HEADS_PER_GROUP])
        max_parts = sb("max_parts", [P, QT, 3, HEADS_PER_GROUP], BF16)
        max_t = [sb(f"max_t{i}", [3 * HEADS_PER_GROUP, SEQ], BF16) for i in range(2)]
        inverse = sb("inverse", [P, UNITS])
        g1 = sb("g1", [P, 1])
        wq = {DECAYED: sb("wq_a", [P, D]), CAUSAL: sb("wq_f", [P, D])}
        wk = {DECAYED: sb("wk_a", [P, D]), CAUSAL: sb("wk_f", [P, D])}
        wv = {DECAYED: sb("wv_a", [P, D]), CAUSAL: sb("wv_f", [P, D])}
        wo = {DECAYED: sb("wo_a", [P, D]), CAUSAL: sb("wo_f", [P, D])}
        wq_rot = sb("wq_rot", [P, HEADS, HD])
        wk_rot = sb("wk_rot", [P, HEADS, HD])
        ones = sb("ones", [P, 1])
        squares = sb("squares", [P, 2])

        def stacked(par, k):
            return near[par][:, k, :, :] if k < 2 else far[:, k - 2, :, :]

        score_a = [pb(f"score_a{i}", [P, SEQ]) for i in range(2)]
        score_b = [pb(f"score_b{i}", [P, 2 * SEQ]) for i in range(2)]
        heads_sum = pb("heads_sum", [P, SEQ])
        bank = pb("bank", [P, SEQ])
        bank_bf = bank[:, :].bitcast(BF16)

        def a_bank(b, g, u, ka, kp):
            if ka == DECAYED or (kp == DECAYED and g < 2):
                return score_a[u % 2], 2
            first = kp == DECAYED and g == 2 and u < 2
            return (score_a + [s[:, 0:SEQ] for s in score_b])[u % 4], 2 if first else 4

        sp_passed, dve_passed, pool_passed = sem("sp_passed"), sem("dve_passed"), sem("pool_passed")
        consts_loaded = sem("consts_loaded")
        wkv_loaded = sem("wkv_loaded")
        dve_setup = sem("dve_setup")
        pool_setup = sem("pool_setup")
        fold_made = sem("fold_made")
        fold_taken = sem("fold_taken")
        squares_summed = sem("squares_summed")
        ones_loaded = sem("ones_loaded")
        rope_loaded = sem("rope_loaded")
        x_loaded = sem("x_loaded")
        bn_done = sem("bn_done")
        moments_ready = sem("moments_ready")
        chain_done = sem("chain_done")
        xn_ready = sem("xn_ready")
        xr_ready = sem("xr_ready")
        xt_made, xt_taken = sem("xt_made"), sem("xt_taken")
        q_made, q_taken = sem("q_made"), sem("q_taken")
        k_made, k_taken = sem("k_made"), sem("k_taken")
        qrot_made, qrot_taken = sem("qrot_made"), sem("qrot_taken")
        krot_made, krot_taken = sem("krot_made"), sem("krot_taken")
        v_made, v_taken = sem("v_made"), sem("v_taken")
        scaled_ready = sem("scaled_ready")
        part0_ready = sem("part0_ready")
        rest_ready = sem("rest_ready")
        part1_ready = sem("part1_ready")
        part2_ready = sem("part2_ready")
        parts_stored = sem("parts_stored")
        near_loaded, far_loaded = sem("near_loaded"), sem("far_loaded")
        ln_stored = sem("ln_stored")
        a_scored, a_maxed = sem("a_scored"), sem("a_maxed")
        max_chain = sem("max_chain")
        maxt_made, maxt_taken = sem("maxt_made"), sem("maxt_taken")
        max_rows_loaded = sem("max_rows_loaded")
        b_scored, b_exped, b_masked = sem("b_scored"), sem("b_exped"), sem("b_masked")
        pv_done, pv_taken = sem("pv_done"), sem("pv_taken")
        ot_made, ot_taken = sem("ot_made"), sem("ot_taken")
        inverse_ready = sem("inverse_ready")
        oo_made, oo_taken = sem("oo_made"), sem("oo_taken")
        y_made, y_taken = sem("y_made"), sem("y_taken")
        y_bn_done = sem("y_bn_done")
        y_moments_ready = sem("y_moments_ready")
        y_chain = sem("y_chain")
        y_normed = sem("y_normed")
        residual_loaded = sem("residual_loaded")
        y_ready = sem("y_ready")
        y_stored = sem("y_stored")

        block = ctx.enter_context(nc.Block())

        CONSTS = [(ident, t["ident"]), (g1, t["g1"].rearrange("(d a) -> d a", a=1)),
                  (wq[DECAYED], t["Wq"]), (wo[DECAYED], t["Wo"]),
                  (wq[CAUSAL], t["wq"]), (wk[CAUSAL], t["wk"]), (wv[CAUSAL], t["wv"]),
                  (wo[CAUSAL], t["wo"]), (grow, t["grow" if decayed else "cosines"]),
                  (shrink, t["shrink" if decayed else "sines"]),
                  (decay, t["decay"]), (causal, t["causal"])]
        wk_in, wv_in = xr[:, 0, :], xr[:, 1, :]
        up_k, up_v = xr[0:LATENT, 2, :], xr[0:LATENT, 3, :]
        down = y[:, 0, 0:LATENT]
        wkv, wkv_t = y[:, 1, :], y[:, 2, :]
        down_t = y[0:LATENT, 3, :]

        @block.sync
        def _(sp):
            for dst, src in () if not decayed else ((wk_in, t["Wk"]), (wv_in, t["Wv"]), (up_k, t["Up_k"]), (up_v, t["Up_v"]),
                             (down, t["Down"])):
                sp.dma_start(dst, src).then_inc(wkv_loaded, 16)
            for dst, src in CONSTS:
                sp.dma_start(dst[:, :], src).then_inc(consts_loaded, 16)
            wait_apart(sp, sp_passed, pool_setup, 2)
            wait_apart(sp, sp_passed, dve_setup, 2)
            for keys in (stacked(0, K_DOWN), stacked(1, K_DOWN), stacked(0, K_UP)):
                sp.dma_start(keys[MAX_ROW:MAX_ROW + 3, :, :],
                             ones3[:, :].unsqueeze(1).to_broadcast([3, HEADS, SEQ])).then_inc(ones_loaded, 16)
            wait_apart(sp, sp_passed, ones_loaded, 48)

            def load_max_rows(grp):
                b, g, par, kind = grp
                s = GROUPS * b + g
                wait_apart(sp, sp_passed, maxt_taken, s + 1)
                h = HEADS_PER_GROUP * g
                for q in (Q_UP, Q_DOWN)[:1 if kind == CAUSAL else 2]:
                    for i in range(3):
                        sp.dma_start(stacked(par, q)[MAX_ROW + i:MAX_ROW + i + 1, h:h + HEADS_PER_GROUP, :],
                                     max_t[g % 2][HEADS_PER_GROUP * i:HEADS_PER_GROUP * (i + 1), :])\
                          .then_inc(max_rows_loaded, 16)

            def store_parts(p, kind, par, i):
                wait_apart(sp, sp_passed, part2_ready, tensors_before(p, kind) + i + 1)
                k = STACKS[kind][i]
                dst = t["scratch"][par, k].rearrange("h d n s -> (h d) n s")
                for first, end, part in Q_RUNS if k in (Q_UP, Q_DOWN) else K_RUNS:
                    n = end - first
                    src = parts[:, i, 0:n, :] if k in (Q_UP, Q_DOWN) else \
                        parts[:, i, part:part + 1, :].to_broadcast([P, n, SEQ])
                    sp.dma_start(dst[:, first:end, :], src).then_inc(parts_stored, 16)

            def load_stack(par, k, h0, h1, signal):
                src = t["scratch"][par, k, h0:h1].rearrange("h d n s -> (d n) h s")
                sp.dma_start(stacked(par, k)[0:TERM_ROWS, h0:h1, :], src).then_inc(signal, 16)

            def load_near(p, kind, par):
                wait_apart(sp, sp_passed, parts_stored, 48 * (tensors_before(p, kind) + len(STACKS[kind])))
                wait_apart(sp, sp_passed, b_scored, 64 * (p - 1))
                load_stack(par, Q_UP, 0, HEADS, near_loaded)
                load_stack(par, K_DOWN, 0, HEADS, near_loaded)
                sp.dma_start(stacked(par, Q_UP)[MAX_ROW:MAX_ROW + 3, :, :],
                             zeros3[:, :].unsqueeze(1).to_broadcast([3, HEADS, SEQ])).then_inc(near_loaded, 16)

            def load_far(b, g, par):
                wait_apart(sp, sp_passed, b_scored, 64 * (b - 1) + UNITS * (g + 1))
                wait_apart(sp, sp_passed, far_loaded, 16 * FAR_LOADS * (GROUPS * b + g))
                h = HEADS_PER_GROUP * g
                load_stack(par, Q_DOWN, h, h + HEADS_PER_GROUP, far_loaded)
                load_stack(par, K_UP, h, h + HEADS_PER_GROUP, far_loaded)

            def body(b, par, ka, kp, kn):
                p, q = b + 1, b - 1
                if kn:
                    wait_apart(sp, sp_passed, xn_ready, p)
                    wait_apart(sp, sp_passed, y_ready, b - 1)
                    if kn == CAUSAL and decayed:
                        wait_apart(sp, sp_passed, y_stored, 16 * (p - decayed + 1))
                    src = t["x"][p] if kn == DECAYED else t["x1"][p - decayed]
                    sp.dma_start(x_in[:, :, :], src.rearrange("(t p) d -> p t d", p=P)).then_inc(x_loaded, 16)
                if kn == CAUSAL and ka == DECAYED:
                    wait_apart(sp, sp_passed, k_taken, decayed)
                    sp.dma_start(grow[:, :], t["cosines"]).then_inc(rope_loaded, 16)
                    sp.dma_start(shrink[:, :], t["sines"]).then_inc(rope_loaded, 16)
                if kp:
                    load_max_rows(scored(b, 0, par, ka, kp))
                if ka == DECAYED:
                    load_far(b, 1, par)
                if kn == CAUSAL:
                    wait_apart(sp, sp_passed, xn_ready, p + 1)
                    sp.dma_start(t["ln_x1"][p - decayed].rearrange("(t p) d -> p t d", p=P), xn[:, :, :])\
                      .then_inc(ln_stored, 16)
                if ka:
                    load_max_rows(scored(b, 1, par, ka, kp))
                if ka == DECAYED:
                    load_far(b, 2, par)
                if kp:
                    if kn:
                        wait_apart(sp, sp_passed, xn_ready, p + 1)
                    wait_apart(sp, sp_passed, y_ready, q)
                    if kp == CAUSAL:
                        wait_apart(sp, sp_passed, ln_stored, 16 * (q - decayed + 1))
                    src = t["x"][q] if kp == DECAYED else t["ln_x1"][q - decayed]
                    sp.dma_start(residual[:, :, :], src.rearrange("(t p) d -> p t d", p=P))\
                      .then_inc(residual_loaded, 16)
                n = len(STACKS[kn]) if kn else 0
                for i in range(n // 2):
                    store_parts(p, kn, 1 - par, i)
                if ka:
                    load_max_rows(scored(b, 2, par, ka, kp))
                for i in range(n // 2, n):
                    store_parts(p, kn, 1 - par, i)
                if ka == DECAYED:
                    load_far(b, 3, par)
                if kn:
                    load_near(p, kn, 1 - par)
                if ka:
                    load_max_rows(scored(b, 3, par, ka, kp))
                if kn == DECAYED:
                    load_far(p, 0, 1 - par)
                if kp:
                    wait_apart(sp, sp_passed, y_ready, q + 1)
                    dst = t["x1"][q] if kp == DECAYED else t["h"][q - decayed]
                    sp.dma_start(dst.rearrange("(t p) d -> p t d", p=P), y[:, :, :]).then_inc(y_stored, 16)

            run_stream(sp, body)
            wait_apart(sp, sp_passed, y_stored, 16 * batches)
            wait_apart(sp, sp_passed, ln_stored, 16 * BATCH)

        @block.tensor
        def _(pe):
            pe.wait_ge(consts_loaded, 16 * len(CONSTS))
            if decayed:
                pe.wait_ge(dve_setup, 3)
                nc.tensor.transpose(bank[:, 0:P], wkv, ident[:, :]).then_inc(fold_made, 1)
                pe.wait_ge(fold_taken, 1)
                nc.tensor.matmul(bank[0:LATENT, 0:P], down, wkv_t, start=True, stop=True).then_inc(fold_made, 1)
                pe.wait_ge(fold_taken, 2)
                nc.tensor.matmul(bank[:, 0:P], down_t, up_k, start=True, stop=True).then_inc(fold_made, 1)
                pe.wait_ge(fold_taken, 3)
                nc.tensor.matmul(bank[:, 0:P], down_t, up_v, start=True, stop=True).then_inc(fold_made, 1)
                pe.wait_ge(fold_taken, 4)
            pe.wait_ge(dve_setup, 8)
            pe.wait_ge(ones_loaded, 48)
            if decayed:
                pe.wait_ge(dve_setup, 9)
                nc.tensor.matmul(score_a[1][0:1, 0:2], ones[:, :], squares[:, :], start=True, stop=True)\
                  .then_inc(squares_summed, 1)
                pe.wait_ge(dve_setup, 10)

            def score_for_max(b, par, kind, kp, g, u):
                j, qt = divmod(u, QT)
                h, n = HEADS_PER_GROUP * g + j, 64 * b + UNITS * g + u
                ps, ring = a_bank(b, g, u, kind, kp)
                wait(pe, a_maxed, n + 1 - ring)
                if g == 0 and u == 0:
                    pe.wait_ge(near_loaded, 16 * NEAR_LOADS * (b + 1))
                keys = SEQ if kind == DECAYED else P * (qt + 1)
                nc.tensor.matmul(ps[:, 0:keys], stacked(par, Q_UP)[:, h, P * qt:P * (qt + 1)],
                                 stacked(par, K_DOWN)[:, h, 0:keys], start=True, stop=True).then_inc(a_scored, 1)

            def score_minus_max(grp, u):
                b, g, par, kind = grp
                kt, j = divmod(u, HEADS_PER_GROUP)
                h, n = HEADS_PER_GROUP * g + j, 64 * b + UNITS * g + u
                wait(pe, b_exped, n - 1)
                if u == 0:
                    pe.wait_ge(max_rows_loaded, max_loads(b, g, kind))
                    if kind == DECAYED:
                        pe.wait_ge(far_loaded, 16 * FAR_LOADS * (GROUPS * b + g + 1))
                ps, cut = score_b[u % 2], P * (kt + 1)
                keys = slice(P * kt, cut)
                if kind == DECAYED:
                    nc.tensor.matmul(ps[:, SEQ - cut:SEQ], stacked(par, K_DOWN)[:, h, keys],
                                     stacked(par, Q_UP)[:, h, 0:cut], start=True, stop=True)
                    nc.tensor.matmul(ps[:, SEQ:2 * SEQ - P * kt], stacked(par, K_UP)[:, h, keys],
                                     stacked(par, Q_DOWN)[:, h, P * kt:SEQ], start=True, stop=True)\
                      .then_inc(b_scored, 1)
                else:
                    nc.tensor.matmul(ps[:, SEQ:2 * SEQ - P * kt], stacked(par, K_DOWN)[:, h, keys],
                                     stacked(par, Q_UP)[:, h, P * kt:SEQ], start=True, stop=True)\
                      .then_inc(b_scored, 1)

            def sum_values(grp, slot):
                b, g, par, kind = grp
                kt, j = divmod(slot, HEADS_PER_GROUP)
                pe.wait_ge(b_masked, 64 * b + UNITS * g + slot + 1)
                if slot == 0:
                    wait(pe, pv_taken, GROUPS * b + g)
                    pe.wait_ge(v_taken, b + 1)
                cut = P * (kt + 1)
                up = (P * kt, SEQ, cut if kind == DECAYED else 0)
                pieces = [up, (0, cut, 0)] if kind == DECAYED else [up]
                for m, (first, end, at) in enumerate(pieces):
                    last = nc.tensor.matmul(
                        heads_sum[32 * j:32 * j + HD + 1, first:end],
                        values[par][:, kt, HEADS_PER_GROUP * g + j, :],
                        probs[:, slot, at:at + end - first],
                        start=(kt == 0 and m == 0), stop=(kt == QT - 1 and m == len(pieces) - 1))
                if j == HEADS_PER_GROUP - 1:
                    last.then_inc(pv_done, 1)

            def body(b, par, ka, kp, kn):
                p, q = b + 1, b - 1
                free = [(v_taken, b + 1) if ka else (ot_taken, 4 * b - 3) if kp else (fold_taken, 4 if decayed else 0)]

                def take_bank(taken, value):
                    wait(pe, *free[0])
                    free[0] = (taken, value)

                for g in range(GROUPS):
                    now, before = finishing(b, g, par, ka, kp), flushed(b, g, par, ka, kp)
                    maxed = scored(b, g, par, ka, kp)
                    for u in range(UNITS):
                        if maxed and u == MAX_TURN_AT[maxed[3]]:
                            s = GROUPS * maxed[0] + maxed[1]
                            take_bank(maxt_taken, s + 1)
                            pe.wait_ge(max_chain, 5 * (s + 1))
                            for qt in range(QT):
                                last = nc.tensor.transpose(
                                    bank_bf[0:3 * HEADS_PER_GROUP, P * qt:P * (qt + 1)],
                                    max_parts[:, qt, :, :].rearrange("p a j -> p (a j)"), ident_bf[:, :])
                            last.then_inc(maxt_made, 1)
                        if u == 10 and before:
                            s = GROUPS * before[0] + before[1]
                            take_bank(ot_taken, s + 1)
                            pe.wait_ge(pv_taken, s + 1)
                            for qt in range(QT):
                                last = nc.tensor.transpose(bank[:, P * qt:P * (qt + 1)],
                                                           heads_t[:, P * qt:P * (qt + 1)], ident[:, :])
                            last.then_inc(ot_made, 1)
                        if (g, u) == TURN_AT.get(kn):
                            take_bank(xt_taken, p + 1)
                            if kn == DECAYED:
                                pe.wait_ge(xn_ready, p + 1)
                            else:
                                pe.wait_ge(xr_ready, p - decayed + 1)
                            src = xn if kn == DECAYED else xr
                            for qt in range(QT):
                                last = nc.tensor.transpose(bank[:, P * qt:P * (qt + 1)], src[:, qt, :], ident[:, :])
                            last.then_inc(xt_made, 1)
                        if (g, u) == QUERIES_AT.get(kn):
                            take_bank(q_taken, p + 1)
                            pe.wait_ge(xt_taken, p + 1)
                            nc.tensor.matmul(bank[:, :], wq[kn][:, :], x_t[:, :], start=True, stop=True)\
                              .then_inc(q_made, 1)
                        if (g, u) == (1, 8) and kn == CAUSAL:
                            take_bank(qrot_taken, p - decayed + 1)
                            nc.tensor.matmul(bank[:, :], wq_rot[:, :, :].rearrange("p h d -> p (h d)"), x_t[:, :],
                                             start=True, stop=True).then_inc(qrot_made, 1)
                        if (g, u) == (1, 14) and kn:
                            take_bank(k_taken, p + 1)
                            nc.tensor.matmul(bank[:, :], wk[kn][:, :], x_t[:, :], start=True, stop=True)\
                              .then_inc(k_made, 1)
                        if (g, u) == (2, 2) and kn == CAUSAL:
                            take_bank(krot_taken, p - decayed + 1)
                            nc.tensor.matmul(bank[:, :], wk_rot[:, :, :].rearrange("p h d -> p (h d)"), x_t[:, :],
                                             start=True, stop=True).then_inc(krot_made, 1)
                        if (g, u) == (2, 14) and kp:
                            take_bank(oo_taken, q + 1)
                            pe.wait_ge(ot_taken, GROUPS * b)
                            for qt in range(QT):
                                last = nc.tensor.transpose(bank[:, P * qt:P * (qt + 1)],
                                                           o[:, qt, :, :].rearrange("p h d -> p (h d)"), ident[:, :])
                            last.then_inc(oo_made, 1)
                        if (g, u) == (3, 2) and kp:
                            take_bank(y_taken, q + 1)
                            pe.wait_ge(oo_taken, q + 1)
                            for qt in range(QT):
                                last = nc.tensor.matmul(bank[:, P * qt:P * (qt + 1)], o_t[:, P * qt:P * (qt + 1)],
                                                        wo[kp][:, :], start=True, stop=True)
                            last.then_inc(y_made, 1)
                        if (g, u) == (3, 14) and kn:
                            take_bank(v_taken, p + 1)
                            for kt in range(QT):
                                last = nc.tensor.matmul(bank[:, P * kt:P * (kt + 1)], x_t[:, P * kt:P * (kt + 1)],
                                                        wv[kn][:, :], start=True, stop=True)
                            last.then_inc(v_made, 1)
                        if ka:
                            score_for_max(b, par, ka, kp, g, u)
                        if now:
                            score_minus_max(now, u)
                        for slot in SUM_IN_NEXT.get(u, ()) if before else ():
                            sum_values(before, slot)
                        for slot in SUM_IN_SAME.get(u, ()) if now else ():
                            sum_values(now, slot)

            run_stream(pe, body)

        @block.scalar
        def _(act):
            if decayed:
                for n, (dst, src) in enumerate(((wkv_t, bank[:, 0:P]), (down_t, bank[0:LATENT, 0:P]),
                                                (wk[DECAYED][:, :], bank[:, 0:P]), (wv[DECAYED][:, :], bank[:, 0:P]))):
                    act.wait_ge(fold_made, n + 1)
                    nc.scalar.activation(dst, src, ACT.Copy).then_inc(fold_taken, 1)

            def body(b, par, ka, kp, kn):
                p, q = b + 1, b - 1
                for g in range(GROUPS):
                    now, before = finishing(b, g, par, ka, kp), flushed(b, g, par, ka, kp)
                    maxed = scored(b, g, par, ka, kp)
                    for u in range(UNITS):
                        if (g, u) == (3, 3) and kp == DECAYED:
                            act.wait_ge(y_made, q + 1)
                            wait(act, y_stored, 16 * q)
                            nc.scalar.activation(y[:, :, :].rearrange("p t d -> p (t d)"), bank[:, :], ACT.Copy)\
                              .then_inc(y_taken, 1)
                        if u == 6 and before:
                            s = GROUPS * before[0] + before[1]
                            act.wait_ge(pv_done, QT * (s + 1))
                            wait(act, ot_made, s)
                            nc.scalar.activation(heads_t[:, :], heads_sum[:, :], ACT.Copy).then_inc(pv_taken, 1)
                        if now:
                            nb, ng, _, kind = now
                            kt = u // HEADS_PER_GROUP
                            wide = SEQ + P if kind == DECAYED else SEQ - P * kt
                            first = SEQ - P * (kt + 1) if kind == DECAYED else SEQ
                            act.wait_ge(b_scored, 64 * nb + UNITS * ng + u + 1)
                            wait(act, pv_done, 16 * nb + 4 * ng + kt - 3)
                            nc.scalar.activation(probs[:, u, 0:wide], score_b[u % 2][:, first:first + wide],
                                                 ACT.Exp).then_inc(b_exped, 1)
                        if maxed and u == MAX_TURN_AT[maxed[3]]:
                            mb, mg, _, kind = maxed
                            s = GROUPS * mb + mg
                            act.wait_ge(maxt_made, s + 1)
                            if not (isinstance(mb, int) and s < 2):
                                kb = DECAYED if isinstance(mb, int) and s <= GROUPS * decayed + 1 else kind
                                act.wait_ge(max_rows_loaded, max_loads(mb, mg - 2, kb))
                            nc.scalar.activation(max_t[mg % 2][:, :], bank_bf[0:3 * HEADS_PER_GROUP, 0:SEQ], ACT.Copy)\
                              .then_inc(maxt_taken, 1)
                        if (g, u) == TURN_AT.get(kn):
                            act.wait_ge(xt_made, p + 1)
                            wait(act, v_made, p)
                            if kn == DECAYED:
                                nc.scalar.activation(x_t[:, :], bank[:, :], ACT.Copy).then_inc(xt_taken, 1)
                            else:
                                nc.scalar.activation(x_t[:, :], bank[:, :], ACT.Copy, scale=g1[:, 0:1])\
                                  .then_inc(xt_taken, 1)
                        if kn:
                            for i, (sg, su) in enumerate(SPLIT_AT[kn]):
                                n = tensors_before(p, kn) + i
                                if (g, u) == (sg, su):
                                    act.wait_ge(scaled_ready, n + 1)
                                    wait(act, parts_stored, 48 * tensors_before(p, kn))
                                    nc.scalar.activation(parts[:, i, 0, :], scaled[:, i, :], ACT.Copy)\
                                      .then_inc(part0_ready, 1)
                                if (g, u) == (sg, su + 2):
                                    act.wait_ge(rest_ready, n + 1)
                                    nc.scalar.activation(parts[:, i, 1, :], scaled[:, i, :], ACT.Copy)\
                                      .then_inc(part1_ready, 1)
                        if (g, u) == (3, 14) and kn:
                            act.wait_ge(v_made, p + 1)
                            wait(act, pv_done, 16 * b)
                            act.wait_ge(dve_setup, 8)
                            nc.scalar.activation(values[1 - par][:, :, :, 0:HD],
                                                 bank[:, :].rearrange("p (t h d) -> p t h d", t=QT, h=HEADS),
                                                 ACT.Copy).then_inc(v_taken, 1)
                        if (g, u) == (2, 14) and kp:
                            act.wait_ge(oo_made, q + 1)
                            wait(act, y_made, q)
                            nc.scalar.activation(o_t[:, :], bank[:, :], ACT.Copy).then_inc(oo_taken, 1)

            run_stream(act, body)

        @block.vector
        def _(dve):
            def link(n, ins):
                ins.then_inc(dve_setup, 1)
                dve.wait_ge(dve_setup, n)

            link(1, nc.vector.memset(ones3[:, :], 1.0))
            nc.vector.memset(near[0][:, :, :, :].rearrange("p a h n -> p (a h n)").bitcast(F32), 0.0)
            link(2, nc.vector.memset(far[:, :, 0:HEADS // 2, :].rearrange("p a h n -> p a (h n)").bitcast(F32), 0.0))
            if decayed:
                dve.wait_ge(wkv_loaded, 16 * 5)
                link(3, nc.vector.tensor_tensor(wkv, wk_in, wv_in, ALU.add))
            else:
                dve.sem_inc(dve_setup, 1)
            dve.wait_ge(consts_loaded, 16 * len(CONSTS))
            link(4, nc.vector.tensor_copy(ident_bf[:, :], ident[:, :]))
            nc.vector.tensor_scalar(wq[DECAYED][:, :], wq[DECAYED][:, :],
                                    SCALE, None, ALU.mult)
            link(5, nc.vector.tensor_scalar(wq[CAUSAL][:, :], wq[CAUSAL][:, :], HD ** -0.5, None, ALU.mult))
            half = HD // 2
            for rot, w in ((wq_rot, wq[CAUSAL]), (wk_rot, wk[CAUSAL])):
                w3 = w[:, :].rearrange("p (h d) -> p h d", d=HD)
                nc.vector.tensor_scalar(rot[:, :, 0:half], w3[:, :, half:HD], -1.0, None, ALU.mult)
                last = nc.vector.tensor_copy(rot[:, :, half:HD], w3[:, :, 0:half])
            link(6, last)
            nc.vector.memset(heads_sum[:, :], 0.0)
            link(7, nc.vector.memset(values[0][:, :, :, :], 1.0))
            link(8, nc.vector.memset(values[1][:, :, :, :], 1.0))
            if decayed:
                nc.vector.memset(ones[:, :], 1.0)
                dve.wait_ge(fold_taken, 4)
                for i, w in enumerate((wq[DECAYED], wk[DECAYED])):
                    last = nc.vector.tensor_tensor_reduce(out=junk[:, i, 0:D], in0=w[:, :], in1=w[:, :], scale=1.0,
                                                          scalar=0.0, op0=ALU.mult, op1=ALU.add,
                                                          accum_out=squares[:, i:i + 1])
                link(9, last)
                dve.wait_ge(squares_summed, 1)
                link(10, nc.vector.tensor_copy(squares[0:1, :], score_a[1][0:1, 0:2]))
                link(11, nc.vector.tensor_tensor(squares[0:1, 0:1], squares[0:1, 0:1], squares[0:1, 1:2], ALU.mult))
                link(12, nc.vector.tensor_scalar(bounded[:, :], squares[0:1, 0:1], float((CLAMP / 2 / D) ** 2), None,
                                                 ALU.is_lt))

            def body(b, par, ka, kp, kn):
                p, q = b + 1, b - 1
                for g in range(GROUPS):
                    before = flushed(b, g, par, ka, kp)
                    for u in range(UNITS):
                        if (g, u) == (1, 9) and kn == CAUSAL:
                            dve.wait_ge(qrot_made, p - decayed + 1)
                            nc.vector.tensor_tensor(scaled[:, 2, :], bank[:, :], shrink[:, :], ALU.mult)\
                              .then_inc(qrot_taken, 1)
                        if (g, u) == (1, 15) and kn == DECAYED:
                            dve.wait_ge(k_made, p + 1)
                            nc.vector.tensor_tensor(scaled[:, 2, :], bank[:, :], shrink[:, :], ALU.mult)\
                              .then_inc(scaled_ready, 1)
                        if (g, u) == (2, 1) and kn == DECAYED:
                            nc.vector.tensor_tensor(scaled[:, 3, :], bank[:, :], grow[:, :], ALU.mult)\
                              .then_inc(scaled_ready, 1)
                            dve.wait_ge(scaled_ready, 4 * (p + 1))
                            dve.sem_inc(k_taken, 1)
                        if (g, u) == (3, 3) and kp == CAUSAL:
                            dve.wait_ge(y_made, q + 1)
                            wait(dve, y_stored, 16 * q)
                            dve.wait_ge(residual_loaded, 16 * (q + 1))
                            nc.vector.tensor_tensor(y[:, :, :].rearrange("p t d -> p (t d)"), bank[:, :],
                                                    residual[:, :, :].rearrange("p t d -> p (t d)"), ALU.add)\
                              .then_inc(y_taken, 1)
                        if ka:
                            j, qt = divmod(u, QT)
                            s = GROUPS * b + g
                            if u == 0:
                                wait_apart(dve, dve_passed, max_chain, 5 * (s - 3))
                            wait_apart(dve, dve_passed, a_scored, 64 * b + UNITS * g + u + 1)
                            if ka == DECAYED:
                                table, op, keys = decay[:, SEQ - P - P * qt:2 * SEQ - P - P * qt], ALU.mult, SEQ
                            else:
                                keys = P * (qt + 1)
                                table, op = causal[:, SEQ - keys:SEQ], ALU.add
                            ps, _ = a_bank(b, g, u, ka, kp)
                            nc.vector.tensor_tensor_reduce(
                                out=junk[:, u % 4, 0:keys], in0=ps[:, 0:keys], in1=table, scale=1.0, scalar=NEG,
                                op0=op, op1=ALU.max, accum_out=maxima[:, g, qt, j:j + 1]).then_inc(a_maxed, 1)
                        start = 2 if kn == DECAYED else 0
                        if g == 0 and start <= u < start + QT and kn:
                            i = u - start
                            if i == 0:
                                dve.wait_ge(x_loaded, 16 * (p + 1))
                            last = nc.vector.bn_stats(bn[:, i, :], x_in[:, i, :])
                            if i == QT - 1:
                                last.then_inc(bn_done, 1)
                        if (g, u) == (0, start + 4) and kn:
                            wait_apart(dve, dve_passed, bn_done, p + 1)
                            wait_apart(dve, dve_passed, chain_done, prep_chain(p, kn))
                            for i in range(QT):
                                last = nc.vector.bn_aggr(moments[:, i, :], bn[:, i, :])
                            last.then_inc(moments_ready, 1)
                        start = 9
                        if g == 0 and start <= u < start + QT and kn:
                            i = u - start
                            if i == 0:
                                wait_apart(dve, dve_passed, chain_done, prep_chain(p, kn) + PREP_CHAIN[kn])
                                wait(dve, xt_made, p)
                            dst, which = (xn, 0) if kn == DECAYED else (xr, 1)
                            last = nc.vector.tensor_scalar(dst[:, i, :], x_in[:, i, :], moments[:, i, 0:1],
                                                           rstds[:, which, i:i + 1], ALU.subtract, ALU.mult)
                            if i == QT - 1:
                                last.then_inc(xn_ready if kn == DECAYED else xr_ready, 1)
                        if kn == CAUSAL and (g, u) in ((0, 14), (0, 15), (1, 0), (1, 1)):
                            i = (u + 2) % UNITS
                            if i == 0:
                                wait(dve, ln_stored, 16 * (p - decayed))
                                if ka == DECAYED:
                                    dve.wait_ge(xt_made, p)
                            last = nc.vector.tensor_scalar(xn[:, i, :], x_in[:, i, :], moments[:, i, 0:1],
                                                           rstds[:, 0, i:i + 1], ALU.subtract, ALU.mult)
                            if i == QT - 1:
                                last.then_inc(xn_ready, 1)
                        if u == 10 and before:
                            s = GROUPS * before[0] + before[1]
                            dve.wait_ge(ot_made, s + 1)
                            view = bank[:, :].rearrange("p (t j e) -> p t j e", t=QT, j=HEADS_PER_GROUP)
                            inv = inverse[:, :].rearrange("p (t j) -> p t j", t=QT)
                            nc.vector.reciprocal(inv, view[:, :, :, HD]).then_inc(inverse_ready, 1)
                            dve.wait_ge(inverse_ready, s + 1)
                            if before[1] == 0:
                                wait(dve, oo_made, before[0])
                            h = HEADS_PER_GROUP * before[1]
                            nc.vector.tensor_tensor(o[:, :, h:h + HEADS_PER_GROUP, :], view[:, :, :, 0:HD],
                                                    inv.unsqueeze(3).to_broadcast([P, QT, HEADS_PER_GROUP, HD]),
                                                    ALU.mult).then_inc(ot_taken, 1)
                        if (g, u) == QUERIES_AT.get(kn):
                            dve.wait_ge(q_made, p + 1)
                            wait(dve, part2_ready, tensors_before(p, kn))
                            if kn == DECAYED:
                                nc.vector.tensor_tensor(scaled[:, 0, :], bank[:, :], grow[:, :], ALU.mult)\
                                  .then_inc(scaled_ready, 1)
                            else:
                                if ka == DECAYED:
                                    dve.wait_ge(rope_loaded, 32)
                                nc.vector.tensor_tensor(scaled[:, 0, :], bank[:, :], grow[:, :], ALU.mult)\
                                  .then_inc(q_taken, 1)
                        if (g, u) == (1, 5) and kn == DECAYED:
                            nc.vector.tensor_tensor(scaled[:, 1, :], bank[:, :], shrink[:, :], ALU.mult)\
                              .then_inc(scaled_ready, 1)
                            dve.wait_ge(scaled_ready, 4 * p + 2)
                            dve.sem_inc(q_taken, 1)
                        if (g, u) == (1, 14) and kn == CAUSAL:
                            dve.wait_ge(k_made, p + 1)
                            nc.vector.tensor_tensor(scaled[:, 1, :], bank[:, :], grow[:, :], ALU.mult)\
                              .then_inc(k_taken, 1)
                        if (g, u) == (2, 2) and kn == CAUSAL:
                            dve.wait_ge(krot_made, p - decayed + 1)
                            nc.vector.tensor_tensor(scaled[:, 3, :], bank[:, :], shrink[:, :], ALU.mult)\
                              .then_inc(krot_taken, 1)
                        if kn:
                            for i, (sg, su) in enumerate(SPLIT_AT[kn]):
                                if (g, u) == (sg, su + 1):
                                    dve.wait_ge(part0_ready, tensors_before(p, kn) + i + 1)
                                    nc.vector.tensor_tensor(scaled[:, i, :], scaled[:, i, :], parts[:, i, 0, :],
                                                            ALU.subtract).then_inc(rest_ready, 1)
                        if g == 3 and u in (4, 5) and kp == DECAYED:
                            if u == 4:
                                dve.wait_ge(y_taken, q + 1)
                            for i in range(2 * (u - 4), 2 * (u - 3)):
                                last = nc.vector.bn_stats(y_bn[:, i, :], y[:, i, :])
                            if u == 5:
                                last.then_inc(y_bn_done, 1)
                        if (g, u) == (3, 6) and kp == DECAYED:
                            wait_apart(dve, dve_passed, y_bn_done, q + 1)
                            for i in range(QT):
                                last = nc.vector.bn_aggr(y_moments[:, i, :], y_bn[:, i, :])
                            last.then_inc(y_moments_ready, 1)
                        if g == 3 and 7 <= u < 7 + QT and kp == DECAYED:
                            i = u - 7
                            if i == 0:
                                dve.wait_ge(y_chain, 2 * (q + 1))
                            last = nc.vector.tensor_scalar(y[:, i, :], y[:, i, :], y_moments[:, i, 0:1],
                                                           y_rstd[:, i:i + 1], ALU.subtract, ALU.mult)
                            if i == QT - 1:
                                last.then_inc(y_normed, 1)
                        if (g, u) == (3, 6) and kp == CAUSAL:
                            dve.wait_ge(y_taken, q + 1)
                            dve.sem_inc(y_ready, 1)

            run_stream(dve, body)

        @block.gpsimd
        def _(pool):
            nc.gpsimd.memset(zeros3[:, :], 0.0)
            nc.gpsimd.memset(minus_half[:, :], -0.5).then_inc(pool_setup, 1)
            nc.gpsimd.memset(near[1][:, :, :, :].rearrange("p a h n -> p (a h n)").bitcast(F32), 0.0)
            nc.gpsimd.memset(far[:, :, HEADS // 2:HEADS, :].rearrange("p a h n -> p a (h n)").bitcast(F32), 0.0)\
              .then_inc(pool_setup, 1)
            wait_apart(pool, pool_passed, pool_setup, 2)

            def mask(grp, u):
                b, g, _, kind = grp
                kt, j = divmod(u, HEADS_PER_GROUP)
                wait_apart(pool, pool_passed, b_exped, 64 * b + UNITS * g + u + 1)
                tile = probs[:, u, :]
                if kind == DECAYED:
                    low, high = tile[:, P * kt:P * (kt + 1)], tile[:, P * (kt + 1):P * (kt + 2)]
                    nc.gpsimd.affine_select(out=low, in_=low, compare_op=ALU.is_ge, fill=0.0, base=0,
                                            pattern=[[-1, P]], channel_multiplier=1)
                    nc.gpsimd.affine_select(out=high, in_=high, compare_op=ALU.is_ge, fill=0.0, base=-1,
                                            pattern=[[1, P]], channel_multiplier=-1).then_inc(b_masked, 1)
                else:
                    diag = tile[:, 0:P]
                    nc.gpsimd.affine_select(out=diag, in_=diag, compare_op=ALU.is_ge, fill=0.0, base=0,
                                            pattern=[[1, P]], channel_multiplier=-1).then_inc(b_masked, 1)

            def split_maxima(grp):
                b, g, _, _ = grp
                s = GROUPS * b + g
                m, rest, rest2 = maxima[:, g, :, :], minus_max[:, 0, :, :], minus_max[:, 1, :, :]
                part = [max_parts[:, :, i, :] for i in range(3)]
                wait_apart(pool, pool_passed, a_maxed, 64 * b + UNITS * (g + 1))
                nc.gpsimd.tensor_scalar(rest, m, -1.0, None, ALU.mult).then_inc(max_chain, 1)
                wait_apart(pool, pool_passed, max_chain, 5 * s + 1)
                wait_apart(pool, pool_passed, maxt_made, s)
                nc.gpsimd.tensor_copy(part[0], rest).then_inc(max_chain, 1)
                wait_apart(pool, pool_passed, max_chain, 5 * s + 2)
                nc.gpsimd.tensor_tensor(rest2, rest, part[0], ALU.subtract).then_inc(max_chain, 1)
                wait_apart(pool, pool_passed, max_chain, 5 * s + 3)
                nc.gpsimd.tensor_copy(part[1], rest2).then_inc(max_chain, 1)
                wait_apart(pool, pool_passed, max_chain, 5 * s + 4)
                nc.gpsimd.tensor_tensor(part[2], rest2, part[1], ALU.subtract).then_inc(max_chain, 1)

            def body(b, par, ka, kp, kn):
                p, q = b + 1, b - 1
                for g in range(GROUPS):
                    now = finishing(b, g, par, ka, kp)
                    maxed = scored(b, g, par, ka, kp)
                    if maxed:
                        split_maxima(maxed)
                    for u in range(UNITS):
                        if now:
                            mask(now, u)
                        if (g, u) == (0, 6 if kn == DECAYED else 4) and kn:
                            c = prep_chain(p, kn)
                            wait_apart(pool, pool_passed, moments_ready, p + 1)
                            wait_apart(pool, pool_passed, xn_ready, p)
                            var = moments[:, :, 1]
                            if kn == DECAYED:
                                nc.gpsimd.tensor_scalar(small[:, 0, :], var, LN_EPS, None, ALU.add)\
                                  .then_inc(chain_done, 1)
                                wait_apart(pool, pool_passed, chain_done, c + 1)
                                nc.gpsimd.tensor_tensor(rstds[:, 0, :], small[:, 0, :], minus_half[:, 0:QT], ALU.pow)\
                                  .then_inc(chain_done, 1)
                            else:
                                nc.gpsimd.tensor_scalar(small[:, 0, :], var, LN_EPS, None, ALU.add)\
                                  .then_inc(chain_done, 1)
                                nc.gpsimd.tensor_scalar(small[:, 1, :], var, 1.0 + RMS_EPS, RMS_EPS * LN_EPS,
                                                        ALU.mult, ALU.add).then_inc(chain_done, 1)
                                wait_apart(pool, pool_passed, chain_done, c + 2)
                                nc.gpsimd.tensor_tensor(rstds[:, :, :].rearrange("p a t -> p (a t)"),
                                                        small[:, :, :].rearrange("p a t -> p (a t)"),
                                                        minus_half[:, :], ALU.pow).then_inc(chain_done, 1)
                        if (g, u) == (1, 9) and kn == CAUSAL:
                            wait_apart(pool, pool_passed, qrot_taken, p - decayed + 1)
                            nc.gpsimd.tensor_tensor(scaled[:, 0, :], scaled[:, 0, :], scaled[:, 2, :], ALU.add)\
                              .then_inc(scaled_ready, 1)
                        if (g, u) == (2, 3) and kn == CAUSAL:
                            wait_apart(pool, pool_passed, krot_taken, p - decayed + 1)
                            nc.gpsimd.tensor_tensor(scaled[:, 1, :], scaled[:, 1, :], scaled[:, 3, :], ALU.add)\
                              .then_inc(scaled_ready, 1)
                        if kn:
                            for i, (sg, su) in enumerate(SPLIT_AT[kn]):
                                if (g, u) == (sg, su + 3):
                                    wait_apart(pool, pool_passed, part1_ready, tensors_before(p, kn) + i + 1)
                                    nc.gpsimd.tensor_tensor(parts[:, i, 2, :], scaled[:, i, :], parts[:, i, 1, :],
                                                            ALU.subtract).then_inc(part2_ready, 1)
                        if (g, u) == (3, 6) and kp == DECAYED:
                            wait_apart(pool, pool_passed, y_moments_ready, q + 1)
                            nc.gpsimd.tensor_scalar(y_small[:, :], y_moments[:, :, 1], LN_EPS, None, ALU.add)\
                              .then_inc(y_chain, 1)
                            wait_apart(pool, pool_passed, y_chain, 2 * q + 1)
                            nc.gpsimd.tensor_tensor(y_rstd[:, :], y_small[:, :], minus_half[:, 0:QT], ALU.pow)\
                              .then_inc(y_chain, 1)
                        if (g, u) == (3, 10) and kp == DECAYED:
                            wait_apart(pool, pool_passed, y_normed, q + 1)
                            wait_apart(pool, pool_passed, residual_loaded, 16 * (q + 1))
                            nc.gpsimd.tensor_tensor(y[:, :, :], y[:, :, :], residual[:, :, :], ALU.add)\
                              .then_inc(y_ready, 1)

            run_stream(pool, body)


HI, LO = 0, 1
PRODUCTS = [(HI, HI), (HI, LO), (LO, HI)]


def experts_program(nc, t):
    ctx = ExitStack()
    with ctx:
        def sb(name, shape, dt=F32):
            return ctx.enter_context(nc.sbuf_tensor(name, shape, dt))

        def pb(name, shape, dt=F32):
            return ctx.enter_context(nc.psum_tensor(name, shape, dt))

        def sem(name):
            return ctx.enter_context(nc.semaphore(name))

        whole_gate = sb("whole_gate", [P, EXPERTS, HIDDEN])
        whole_up = sb("whole_up", [P, EXPERTS, HIDDEN])
        w_gate = sb("w_gate", [P, 2, EXPERTS, HIDDEN])
        w_up = sb("w_up", [P, 2, EXPERTS, HIDDEN])
        w_down = sb("w_down", [P, EXPERTS, HC, D])
        router = sb("router", [P, EXPERTS])
        g2 = sb("g2", [P, 1])
        eye = sb("eye", [P, P])
        lower = sb("lower", [P, EXPERTS, EXPERTS])
        half = sb("half", [P, QT])
        h_in = [sb(f"h_in{i}", [P, QT, D]) for i in range(2)]
        hn = sb("hn", [P, QT, D])
        h_t = [sb(f"h_t{i}", [P, SEQ]) for i in range(2)]
        h_parts = [sb(f"h_parts{i}", [P, 2, SEQ]) for i in range(2)]
        x1 = [sb(f"x1_{i}", [P, QT, D]) for i in range(2)]
        gated = [sb(f"gated{i}", [P, SEQ]) for i in range(2)]
        hidden = [sb(f"hidden{i}", [P, HC, SEQ]) for i in range(2)]
        acc = [sb(f"acc{i}", [P, QT, D]) for i in range(2)]
        weight = [sb(f"weight{i}", [P, QT, EXPERTS]) for i in range(2)]
        bn = sb("h_bn", [P, QT, 6])
        mom = sb("h_moments", [P, QT, 2])
        square = sb("square", [P, QT])
        rms = sb("h_rms", [P, QT])
        bn2 = sb("out_bn", [P, QT, 6])
        mom2 = sb("out_moments", [P, QT, 2])
        small2 = sb("out_small", [P, QT])
        rstd2 = sb("out_rstd", [P, QT])
        top = sb("top", [P, QT])
        e_in = sb("e_in", [P, QT, EXPERTS])
        e = sb("e", [P, QT, EXPERTS])
        greater = sb("greater", [P, QT, EXPERTS, EXPERTS])
        ties = sb("ties", [P, QT, EXPERTS, EXPERTS])
        rank = sb("rank", [P, QT, EXPERTS])
        total = sb("total", [P, QT])

        gate_ps = [pb(f"gate_ps{i}", [P, SEQ]) for i in range(2)]
        up_ps = [pb(f"up_ps{i}", [P, SEQ]) for i in range(2)]
        down_ps = [pb(f"down_ps{i}", [P, QT, D]) for i in range(2)]
        turn_ps = pb("turn_ps", [P, SEQ])
        logits = pb("logits", [P, QT, EXPERTS])

        weights_loaded = sem("weights_loaded")
        upper_made, weights_split = sem("upper_made"), sem("weights_split")
        h_upper_made, h_split = sem("h_upper_made"), sem("h_split")
        expert_loaded = [sem(f"expert_loaded{x}") for x in range(EXPERTS)]
        sp_passed, dve_passed, pool_passed = sem("moe_sp_passed"), sem("moe_dve_passed"), sem("moe_pool_passed")
        half_ready = sem("half_ready")
        h_loaded = sem("h_loaded")
        prep_dve = sem("prep_dve")
        rms_chain = sem("rms_chain")
        total_ready = sem("total_ready")
        hn_ready = sem("hn_ready")
        ht_made, ht_taken = sem("ht_made"), sem("ht_taken")
        logits_made = sem("logits_made")
        route_a = sem("route_a")
        e_ready = sem("e_ready")
        route_b = sem("route_b")
        gate_made, gate_taken = sem("gate_made"), sem("gate_taken")
        up_made, hidden_made = sem("up_made"), sem("hidden_made")
        down_made, down_taken = sem("down_made"), sem("down_taken")
        out_dve = sem("out_dve")
        out_chain = sem("out_chain")
        out_normed = sem("out_normed")
        x1_loaded = sem("x1_loaded")
        out_ready = sem("out_ready")
        out_stored = sem("out_stored")

        block = ctx.enter_context(nc.Block())
        NW = 4
        ROUTE = 8

        def rows(tensor, n):
            return tensor[n].rearrange("(t p) d -> p t d", p=P)

        def after_first(n):
            return not isinstance(n, int) or n > 0

        def run_groups(eng, body):
            body(-1, 1, True)
            body(0, 0, True)
            body(1, 1, True)
            body(2, 0, True)
            with eng.Fori(0, (BATCH - 4) // 2) as i:
                body(2 * i + 3, 1, True)
                body(2 * i + 4, 0, True)
            body(BATCH - 1, 1, False)

        @block.sync
        def _(sp):
            sp.dma_start(h_in[0][:, :, :], rows(t["h"], 0)).then_inc(h_loaded, 16)
            sp.dma_start(eye[:, :], t["ident"]).then_inc(weights_loaded, 16)
            sp.dma_start(g2[:, :], t["g2"].rearrange("(d a) -> d a", a=1)).then_inc(weights_loaded, 16)
            sp.dma_start(router[:, :], t["w_router"]).then_inc(weights_loaded, 16)
            sp.dma_start(lower[:, :, :], t["lower"]).then_inc(weights_loaded, 16)
            for x in range(EXPERTS):
                sp.dma_start(whole_gate[:, x, :], t["wg"][x]).then_inc(expert_loaded[x], 16)
                sp.dma_start(whole_up[:, x, :], t["wu"][x]).then_inc(expert_loaded[x], 16)
                sp.dma_start(w_down[:, x, :, :], t["wd"][x].rearrange("(c p) d -> p c d", p=P))\
                  .then_inc(expert_loaded[x], 16)

            def body(n, par, more):
                real = not (isinstance(n, int) and n < 0)
                if real:
                    wait_apart(sp, sp_passed, out_ready, n - 1)
                    wait_apart(sp, sp_passed, x1_loaded, 16 * n)
                    sp.dma_start(x1[par][:, :, :], rows(t["x1"], n)).then_inc(x1_loaded, 16)
                if more and real:
                    wait_apart(sp, sp_passed, down_taken, EXPERTS * n)
                    wait_apart(sp, sp_passed, h_loaded, 16 * (n + 1))
                    sp.dma_start(h_in[1 - par][:, :, :], rows(t["h"], n + 1)).then_inc(h_loaded, 16)
                for m, m_par in ([(n - 1, 1 - par)] if after_first(n) else []) + ([] if more else [(n, par)]):
                    wait_apart(sp, sp_passed, out_ready, m + 1)
                    sp.dma_start(rows(t["out"], m), acc[m_par][:, :, :]).then_inc(out_stored, 16)

            run_groups(sp, body)
            wait_apart(sp, sp_passed, out_stored, 16 * BATCH)

        @block.tensor
        def _(pe):
            pe.wait_ge(weights_loaded, 16 * NW)

            def product(out, w, x, c, par):
                for m, (w_part, h_part) in enumerate(PRODUCTS):
                    last = nc.tensor.matmul(out[:, :], w[:, w_part, x, P * c:P * (c + 1)].bitcast(F32R),
                                            h_parts[par][:, h_part, :].bitcast(F32R),
                                            start=(m == 0), stop=(m == len(PRODUCTS) - 1))
                return last

            def down(n, par, x):
                m = EXPERTS * n + x
                pe.wait_ge(hidden_made, HC * (m + 1))
                wait(pe, down_taken, m - 1)
                for qt in range(QT):
                    for c in range(HC):
                        last = nc.tensor.matmul(down_ps[x % 2][:, qt, :], hidden[x % 2][:, c, P * qt:P * (qt + 1)],
                                                w_down[:, x, c, :], start=(c == 0), stop=(c == HC - 1))
                last.then_inc(down_made, 1)

            def body(n, par, more):
                real = not (isinstance(n, int) and n < 0)
                for x in range(EXPERTS):
                    if x == 2 and more:
                        pe.wait_ge(hn_ready, n + 2)
                        wait(pe, ht_taken, n + 1)
                        for qt in range(QT):
                            last = nc.tensor.transpose(turn_ps[:, P * qt:P * (qt + 1)], hn[:, qt, :], eye[:, :])
                        last.then_inc(ht_made, 1)
                    if x == 4 and more:
                        pe.wait_ge(ht_taken, n + 2)
                        wait(pe, route_a, 2 * (n + 1))
                        for qt in range(QT):
                            last = nc.tensor.matmul(logits[:, qt, :], h_t[1 - par][:, P * qt:P * (qt + 1)],
                                                    router[:, :], start=True, stop=True)
                        last.then_inc(logits_made, 1)
                    if not real:
                        continue
                    if x == 0:
                        pe.wait_ge(h_split, n + 1)
                    if isinstance(n, int) and n == 0:
                        pe.wait_ge(expert_loaded[x], 48)
                        pe.wait_ge(weights_split, x + 1)
                    for c in range(HC):
                        k = HC * (EXPERTS * n + x) + c
                        wait(pe, gate_taken, k - 1)
                        product(gate_ps[(HC * x + c) % 2], w_gate, x, c, par).then_inc(gate_made, 1)
                        wait(pe, hidden_made, k - 1)
                        product(up_ps[(HC * x + c) % 2], w_up, x, c, par).then_inc(up_made, 1)
                    if x > 0:
                        down(n, par, x - 1)
                if real:
                    down(n, par, EXPERTS - 1)

            run_groups(pe, body)

        @block.scalar
        def _(act):
            act.wait_ge(weights_loaded, 16 * NW)

            def body(n, par, more):
                real = not (isinstance(n, int) and n < 0)
                for x in range(EXPERTS):
                    if x == 2 and more:
                        act.wait_ge(ht_made, n + 2)
                        wait(act, down_made, EXPERTS * n)
                        nc.scalar.activation(h_t[1 - par][:, :], turn_ps[:, :], ACT.Copy, scale=g2[:, 0:1])\
                          .then_inc(ht_taken, 1)
                    if x == 5 and more:
                        act.wait_ge(route_a, 2 * (n + 2))
                        wait(act, route_b, ROUTE * (n + 1))
                        nc.scalar.activation(e[:, :, :], e_in[:, :, :], ACT.Exp).then_inc(e_ready, 1)
                    if not real:
                        continue
                    for c in range(HC):
                        k = HC * (EXPERTS * n + x) + c
                        act.wait_ge(gate_made, k + 1)
                        wait(act, hidden_made, k - 1)
                        nc.scalar.activation(gated[(HC * x + c) % 2][:, :], gate_ps[(HC * x + c) % 2][:, :], ACT.Silu)\
                          .then_inc(gate_taken, 1)

            run_groups(act, body)

        @block.vector
        def _(dve):
            def split_weights(x):
                dve.wait_ge(expert_loaded[x], 48)
                for w, whole in ((w_gate, whole_gate), (w_up, whole_up)):
                    last = nc.vector.tensor_copy(w[:, HI, x, :].bitcast(F32R), whole[:, x, :])
                last.then_inc(upper_made, 1)
                dve.wait_ge(upper_made, x + 1)
                for w, whole in ((w_gate, whole_gate), (w_up, whole_up)):
                    last = nc.vector.tensor_tensor(w[:, LO, x, :].bitcast(F32R), whole[:, x, :], w[:, HI, x, :],
                                                   ALU.subtract)
                last.then_inc(weights_split, 1)

            def route(n, par, x, c):
                k = ROUTE * (n + 1)
                wide = [P, QT, EXPERTS, EXPERTS]
                if (x, c) == (6, 0):
                    if isinstance(n, int) and n < 0:
                        dve.wait_ge(weights_loaded, 16 * NW)
                    dve.wait_ge(e_ready, n + 2)
                    other, own = e[:, :, :].unsqueeze(2).to_broadcast(wide), e[:, :, :].unsqueeze(3).to_broadcast(wide)
                    nc.vector.tensor_tensor(greater[:, :, :, :], other, own, ALU.is_gt).then_inc(route_b, 1)
                    nc.vector.tensor_tensor(ties[:, :, :, :], other, own, ALU.is_equal).then_inc(route_b, 1)
                if (x, c) == (6, 1):
                    dve.wait_ge(route_b, k + 2)
                    nc.vector.tensor_tensor(ties[:, :, :, :], ties[:, :, :, :],
                                            lower[:, :, :].unsqueeze(1).to_broadcast(wide), ALU.mult)\
                      .then_inc(route_b, 1)
                    dve.wait_ge(route_b, k + 3)
                    nc.vector.tensor_tensor(ties[:, :, :, :], ties[:, :, :, :], greater[:, :, :, :], ALU.add)\
                      .then_inc(route_b, 1)
                if (x, c) == (6, 2):
                    dve.wait_ge(route_b, k + 4)
                    nc.vector.reduce_sum(rank[:, :, :], ties[:, :, :, :], AX.X).then_inc(route_b, 1)
                    dve.wait_ge(route_b, k + 5)
                    nc.vector.scalar_tensor_tensor(out=rank[:, :, :], in0=rank[:, :, :], scalar=1.5,
                                                   in1=e[:, :, :], op0=ALU.is_lt, op1=ALU.mult)\
                      .then_inc(route_b, 1)
                if (x, c) == (7, 0):
                    dve.wait_ge(route_b, k + 6)
                    nc.vector.reduce_sum(total[:, :], rank[:, :, :], AX.X).then_inc(total_ready, 1)
                    dve.wait_ge(total_ready, n + 2)
                    nc.vector.reciprocal(total[:, :], total[:, :]).then_inc(route_b, 1)
                    dve.wait_ge(route_b, k + 7)
                    nc.vector.tensor_tensor(weight[1 - par][:, :, :], rank[:, :, :],
                                            total[:, :].unsqueeze(2).to_broadcast([P, QT, EXPERTS]), ALU.mult)\
                      .then_inc(route_b, 1)

            def normalise(n, par):
                dve.wait_ge(out_chain, 2 * (n + 1))
                for i in range(QT):
                    last = nc.vector.tensor_scalar(acc[par][:, i, :], acc[par][:, i, :], mom2[:, i, 0:1],
                                                   rstd2[:, i:i + 1], ALU.subtract, ALU.mult)
                last.then_inc(out_normed, 1)

            def body(n, par, more):
                real = not (isinstance(n, int) and n < 0)

                def add_up(x):
                    m = EXPERTS * n + x
                    dve.wait_ge(down_made, m + 1)
                    if x == 0:
                        dve.wait_ge(route_b, ROUTE * (n + 1))
                        wait(dve, out_stored, 16 * (n - 1))
                    else:
                        dve.wait_ge(down_taken, m)
                    for qt in range(QT):
                        last = nc.vector.scalar_tensor_tensor(
                            out=acc[par][:, qt, :], in0=down_ps[x % 2][:, qt, :], scalar=weight[par][:, qt, x:x + 1],
                            in1=(h_in if x == 0 else acc)[par][:, qt, :], op0=ALU.mult, op1=ALU.add)
                    last.then_inc(down_taken, 1)

                for x in range(EXPERTS):
                    if x == 2 and after_first(n):
                        normalise(n - 1, 1 - par)
                    if x == 3 and more:
                        dve.wait_ge(ht_taken, n + 2)
                        wait(dve, down_made, EXPERTS * n)
                        nc.vector.tensor_copy(h_parts[1 - par][:, HI, :].bitcast(F32R), h_t[1 - par][:, :])\
                          .then_inc(h_upper_made, 1)
                    if x == 5 and more:
                        dve.wait_ge(h_upper_made, n + 2)
                        nc.vector.tensor_tensor(h_parts[1 - par][:, LO, :].bitcast(F32R), h_t[1 - par][:, :],
                                                h_parts[1 - par][:, HI, :], ALU.subtract).then_inc(h_split, 1)
                    if x == EXPERTS - 1 and not real:
                        split_weights(0)
                    if isinstance(n, int) and n == 0 and x < EXPERTS - 1:
                        split_weights(x + 1)
                    if x == 1 and more:
                        dve.wait_ge(h_loaded, 16 * (n + 2))
                        for i in range(QT):
                            last = nc.vector.bn_stats(bn[:, i, :], h_in[1 - par][:, i, :])
                        last.then_inc(prep_dve, 1)
                        wait_apart(dve, dve_passed, prep_dve, 2 * (n + 1) + 1)
                        for i in range(QT):
                            last = nc.vector.bn_aggr(mom[:, i, :], bn[:, i, :])
                        last.then_inc(prep_dve, 1)
                    if x == 4 and more:
                        k = 2 * (n + 1)
                        dve.wait_ge(logits_made, n + 2)
                        nc.vector.reduce_max(top[:, :], logits[:, :, :], AX.X).then_inc(route_a, 1)
                        dve.wait_ge(route_a, k + 1)
                        nc.vector.tensor_tensor(e_in[:, :, :], logits[:, :, :],
                                                top[:, :].unsqueeze(2).to_broadcast([P, QT, EXPERTS]), ALU.subtract)\
                          .then_inc(route_a, 1)
                    for c in range(HC):
                        if more:
                            route(n, par, x, c)
                        if not real:
                            continue
                        k = HC * (EXPERTS * n + x) + c
                        dve.wait_ge(up_made, k + 1)
                        dve.wait_ge(gate_taken, k + 1)
                        if c == 0:
                            wait(dve, down_made, EXPERTS * n + x - 1)
                        nc.vector.tensor_tensor(hidden[x % 2][:, c, :], up_ps[(HC * x + c) % 2][:, :],
                                                gated[(HC * x + c) % 2][:, :], ALU.mult).then_inc(hidden_made, 1)
                    if x > 0 and real:
                        add_up(x - 1)
                if real:
                    add_up(EXPERTS - 1)
                    dve.wait_ge(down_taken, EXPERTS * (n + 1))
                    for i in range(QT):
                        last = nc.vector.bn_stats(bn2[:, i, :], acc[par][:, i, :])
                    last.then_inc(out_dve, 1)
                    wait_apart(dve, dve_passed, out_dve, 2 * n + 1)
                    for i in range(QT):
                        last = nc.vector.bn_aggr(mom2[:, i, :], bn2[:, i, :])
                    last.then_inc(out_dve, 1)
                    if not more:
                        normalise(n, par)

            run_groups(dve, body)

        @block.gpsimd
        def _(pool):
            nc.gpsimd.memset(half[:, :], -0.5).then_inc(half_ready, 1)
            wait_apart(pool, pool_passed, half_ready, 1)

            def finish(n, par):
                wait_apart(pool, pool_passed, out_normed, n + 1)
                wait_apart(pool, pool_passed, x1_loaded, 16 * (n + 1))
                nc.gpsimd.tensor_tensor(acc[par][:, :, :], acc[par][:, :, :], x1[par][:, :, :], ALU.add)\
                  .then_inc(out_ready, 1)

            def body(n, par, more):
                real = not (isinstance(n, int) and n < 0)
                if more:
                    k = 4 * (n + 1)
                    wait_apart(pool, pool_passed, prep_dve, 2 * (n + 2))
                    nc.gpsimd.tensor_tensor(square[:, :], mom[:, :, 0], mom[:, :, 0], ALU.mult).then_inc(rms_chain, 1)
                    wait_apart(pool, pool_passed, rms_chain, k + 1)
                    nc.gpsimd.tensor_tensor(square[:, :], square[:, :], mom[:, :, 1], ALU.add).then_inc(rms_chain, 1)
                    wait_apart(pool, pool_passed, rms_chain, k + 2)
                    nc.gpsimd.tensor_scalar(square[:, :], square[:, :], RMS_EPS, None, ALU.add).then_inc(rms_chain, 1)
                    wait_apart(pool, pool_passed, rms_chain, k + 3)
                    nc.gpsimd.tensor_tensor(rms[:, :], square[:, :], half[:, :], ALU.pow).then_inc(rms_chain, 1)
                    wait_apart(pool, pool_passed, rms_chain, k + 4)
                    wait_apart(pool, pool_passed, ht_made, n + 1)
                    nc.gpsimd.tensor_tensor(hn[:, :, :], h_in[1 - par][:, :, :],
                                            rms[:, :].unsqueeze(2).to_broadcast([P, QT, D]), ALU.mult)\
                      .then_inc(hn_ready, 1)
                if after_first(n):
                    finish(n - 1, 1 - par)
                if real:
                    wait_apart(pool, pool_passed, out_dve, 2 * (n + 1))
                    nc.gpsimd.tensor_scalar(small2[:, :], mom2[:, :, 1], LN_EPS, None, ALU.add).then_inc(out_chain, 1)
                    wait_apart(pool, pool_passed, out_chain, 2 * n + 1)
                    nc.gpsimd.tensor_tensor(rstd2[:, :], small2[:, :], half[:, :], ALU.pow).then_inc(out_chain, 1)
                    if not more:
                        finish(n, par)

            run_groups(pool, body)


def clipped_attention_program(nc, t, sems):
    ctx = ExitStack()
    with ctx:
        def sb(name, shape, dt=F32):
            return ctx.enter_context(nc.sbuf_tensor("c_" + name, shape, dt))

        def pb(name, shape, dt=F32):
            return ctx.enter_context(nc.psum_tensor("c_" + name, shape, dt))

        def sem(name):
            return ctx.enter_context(nc.semaphore("c_" + name))

        ident = sb("ident", [P, P])
        true_decay = sb("true_decay", [P, 2 * SEQ - P])
        wq, wk, wv, wo = (sb(name, [P, D]) for name in ("wq", "wk", "wv", "wo"))
        wkv = sb("wkv", [P, D])
        w_down = sb("w_down", [P, LATENT])
        up_k, up_v = sb("up_k", [LATENT, D]), sb("up_v", [LATENT, D])
        half = sb("half", [P, QT])
        x_in, xn, y, v = (sb(name, [P, QT, D]) for name in ("x_in", "xn", "y", "v"))
        x_t, q_t, sum_t, k_t, o_t = (sb(name, [P, SEQ]) for name in ("x_t", "q_t", "sum_t", "k_t", "o_t"))
        latent_t = sb("latent_t", [LATENT, SEQ])
        bn, mom = sb("bn", [P, QT, 6]), sb("mom", [P, QT, 2])
        small, rstd = sb("small", [P, QT]), sb("rstd", [P, QT])
        q_h, k_h = sb("q_h", [HD, SEQ]), sb("k_h", [HD, SEQ])
        v_h, o_h = sb("v_h", [P, QT, HD]), sb("o_h", [P, QT, HD])
        o = sb("o", [P, QT, D])
        probs = sb("probs", [P, SEQ])
        probs_t = sb("probs_t", [P, QT, P])
        top, total, share = sb("top", [P, 1]), sb("total", [P, 1]), sb("share", [P, 1])

        turn_ps, q_ps, wide_ps, v_ps = (pb(name, [P, SEQ]) for name in ("turn_ps", "q_ps", "wide_ps", "v_ps"))
        latent_ps = pb("latent_ps", [LATENT, SEQ])
        score_ps = pb("score_ps", [P, SEQ])
        o_ps = pb("o_ps", [P, QT, HD])

        sp_passed, dve_passed, pool_passed = sem("sp_passed"), sem("dve_passed"), sem("pool_passed")
        consts_loaded, weights_added, half_ready = sem("consts_loaded"), sem("weights_added"), sem("half_ready")
        batch_free = sem("batch_free")
        x_loaded, stats_ready, chain_done = sem("x_loaded"), sem("stats_ready"), sem("chain_done")
        xn_ready = sem("xn_ready")
        turned, turn_taken = sem("turned"), sem("turn_taken")
        projected, projection_taken = sem("projected"), sem("projection_taken")
        projections_stored, head_loaded = sem("projections_stored"), sem("head_loaded")
        scored, softmax_steps, exped = sem("scored"), sem("softmax_steps"), sem("exped")
        probs_turned, turned_taken = sem("probs_turned"), sem("turned_taken")
        head_summed, head_taken, head_stored = sem("head_summed"), sem("head_taken"), sem("head_stored")
        o_loaded = sem("o_loaded")
        y_normed = sem("y_normed")
        y_made, y_taken = sem("y_made"), sem("y_taken")
        y_ready, x1_stored = sem("y_ready"), sem("x1_stored")
        STEPS = 8

        block = ctx.enter_context(nc.Block())
        CONSTS = [(ident, t["ident"]), (true_decay, t["true_decay"]), (wq, t["Wq"]), (wk, t["Wk"]), (wv, t["Wv"]),
                  (wo, t["Wo"]), (w_down, t["Down"]), (up_k, t["Up_k"]), (up_v, t["Up_v"])]

        def each_batch(eng, before, head, after):
            with eng.Fori(0, BATCH) as b:
                before(b)
                if head:
                    with eng.Fori(0, HEADS) as h:
                        head(b, h, b * HEADS + h)
                after(b)

        @block.sync
        def _(sp):
            for dst, src in CONSTS:
                sp.dma_start(dst[:, :], src).then_inc(consts_loaded, 16)
            sp.sem_inc(batch_free, 1)

            def before(b):
                wait_apart(sp, sp_passed, batch_free, b + 1)
                sp.dma_start(x_in[:, :, :], t["x"][b].rearrange("(t p) d -> p t d", p=P)).then_inc(x_loaded, 16)
                wait_apart(sp, sp_passed, projection_taken, 5 * b + 5)
                sp.dma_start(t["kept_q"], q_t[:, :]).then_inc(projections_stored, 16)
                sp.dma_start(t["kept_k"], k_t[:, :]).then_inc(projections_stored, 16)
                sp.dma_start(t["kept_v"].rearrange("(t p) d -> p t d", p=P), v[:, :, :])\
                  .then_inc(projections_stored, 16)
                wait_apart(sp, sp_passed, projections_stored, 48 * b + 48)

            def head(b, h, n):
                sp.dma_start(q_h[:, :], t["kept_q"].rearrange("(h d) s -> h d s", d=HD)[h]).then_inc(head_loaded, 16)
                sp.dma_start(k_h[:, :], t["kept_k"].rearrange("(h d) s -> h d s", d=HD)[h]).then_inc(head_loaded, 16)
                sp.dma_start(v_h[:, :, :], t["kept_v"].rearrange("(t p) (h d) -> h p t d", p=P, d=HD)[h])\
                  .then_inc(head_loaded, 16)
                wait_apart(sp, sp_passed, head_taken, n + 1)
                sp.dma_start(t["kept_o"].rearrange("(t p) (h d) -> h p t d", p=P, d=HD)[h], o_h[:, :, :])\
                  .then_inc(head_stored, 16)
                wait_apart(sp, sp_passed, head_stored, 16 * n + 16)

            def after(b):
                sp.dma_start(o[:, :, :], t["kept_o"].rearrange("(t p) d -> p t d", p=P)).then_inc(o_loaded, 16)
                wait_apart(sp, sp_passed, y_ready, b + 1)
                sp.dma_start(t["x1"][b].rearrange("(t p) d -> p t d", p=P), y[:, :, :]).then_inc(x1_stored, 16)
                wait_apart(sp, sp_passed, x1_stored, 16 * b + 16)
                sp.sem_inc(batch_free, 1)

            each_batch(sp, before, head, after)
            sp.wait_ge(x1_stored, 16 * BATCH)

        @block.tensor
        def _(pe):
            pe.wait_ge(consts_loaded, 16 * len(CONSTS))
            pe.wait_ge(weights_added, 1)

            def before(b):
                pe.wait_ge(xn_ready, b + 1)
                for i in range(QT):
                    last = nc.tensor.transpose(turn_ps[:, P * i:P * (i + 1)], xn[:, i, :], ident[:, :])
                last.then_inc(turned, 1)
                pe.wait_ge(turn_taken, 2 * b + 1)
                nc.tensor.matmul(q_ps[:, :], wq[:, :], x_t[:, :], start=True, stop=True).then_inc(projected, 1)
                nc.tensor.matmul(wide_ps[:, :], wkv[:, :], x_t[:, :], start=True, stop=True).then_inc(projected, 1)
                pe.wait_ge(projection_taken, 5 * b + 2)
                nc.tensor.matmul(latent_ps[:, :], w_down[:, :], sum_t[:, :], start=True, stop=True)\
                  .then_inc(projected, 1)
                pe.wait_ge(projection_taken, 5 * b + 3)
                nc.tensor.matmul(wide_ps[:, :], up_k[:, :], latent_t[:, :], start=True, stop=True)\
                  .then_inc(projected, 1)
                for i in range(QT):
                    last = nc.tensor.matmul(v_ps[:, P * i:P * (i + 1)], latent_t[:, P * i:P * (i + 1)], up_v[:, :],
                                            start=True, stop=True)
                last.then_inc(projected, 1)

            def head(b, h, n):
                pe.wait_ge(head_loaded, 48 * n + 48)
                for qt in range(QT):
                    m = QT * n + qt
                    nc.tensor.matmul(score_ps[:, :], q_h[:, P * qt:P * (qt + 1)], k_h[:, :], start=True, stop=True)\
                      .then_inc(scored, 1)
                    pe.wait_ge(softmax_steps, STEPS * m + STEPS)
                    for kt in range(QT):
                        last = nc.tensor.transpose(turn_ps[:, P * kt:P * (kt + 1)], probs[:, P * kt:P * (kt + 1)],
                                                   ident[:, :])
                    last.then_inc(probs_turned, 1)
                    pe.wait_ge(turned_taken, m + 1)
                    for kt in range(QT):
                        last = nc.tensor.matmul(o_ps[:, qt, :], probs_t[:, kt, :], v_h[:, kt, :],
                                                start=(kt == 0), stop=(kt == QT - 1))
                last.then_inc(head_summed, 1)

            def after(b):
                pe.wait_ge(o_loaded, 16 * b + 16)
                for i in range(QT):
                    last = nc.tensor.transpose(turn_ps[:, P * i:P * (i + 1)], o[:, i, :], ident[:, :])
                last.then_inc(turned, 1)
                pe.wait_ge(turn_taken, 2 * b + 2)
                for i in range(QT):
                    last = nc.tensor.matmul(wide_ps[:, P * i:P * (i + 1)], o_t[:, P * i:P * (i + 1)], wo[:, :],
                                            start=True, stop=True)
                last.then_inc(y_made, 1)

            each_batch(pe, before, head, after)

        @block.scalar
        def _(act):
            def before(b):
                act.wait_ge(turned, 2 * b + 1)
                nc.scalar.activation(x_t[:, :], turn_ps[:, :], ACT.Copy).then_inc(turn_taken, 1)
                flat_v = v[:, :, :].rearrange("p t d -> p (t d)")
                for i, (dst, src) in enumerate(((q_t[:, :], q_ps[:, :]), (sum_t[:, :], wide_ps[:, :]),
                                                (latent_t[:, :], latent_ps[:, :]), (k_t[:, :], wide_ps[:, :]),
                                                (flat_v, v_ps[:, :]))):
                    act.wait_ge(projected, 5 * b + i + 1)
                    nc.scalar.activation(dst, src, ACT.Copy).then_inc(projection_taken, 1)

            def head(b, h, n):
                for qt in range(QT):
                    m = QT * n + qt
                    act.wait_ge(softmax_steps, STEPS * m + 5)
                    nc.scalar.activation(probs[:, :], probs[:, :], ACT.Exp).then_inc(exped, 1)
                    act.wait_ge(probs_turned, m + 1)
                    nc.scalar.activation(probs_t[:, :, :].rearrange("p t k -> p (t k)"), turn_ps[:, :], ACT.Copy)\
                      .then_inc(turned_taken, 1)
                act.wait_ge(head_summed, n + 1)
                nc.scalar.activation(o_h[:, :, :], o_ps[:, :, :], ACT.Copy).then_inc(head_taken, 1)

            def after(b):
                act.wait_ge(turned, 2 * b + 2)
                nc.scalar.activation(o_t[:, :], turn_ps[:, :], ACT.Copy).then_inc(turn_taken, 1)
                act.wait_ge(y_made, b + 1)
                nc.scalar.activation(y[:, :, :].rearrange("p t d -> p (t d)"), wide_ps[:, :], ACT.Copy)\
                  .then_inc(y_taken, 1)

            each_batch(act, before, head, after)

        @block.vector
        def _(dve):
            dve.wait_ge(consts_loaded, 16 * len(CONSTS))
            nc.vector.tensor_tensor(wkv[:, :], wk[:, :], wv[:, :], ALU.add).then_inc(weights_added, 1)
            dve.wait_ge(half_ready, 1)

            def normalise(dst, src, value, done):
                for i in range(QT):
                    last = nc.vector.bn_stats(bn[:, i, :], src[:, i, :])
                last.then_inc(stats_ready, 1)
                wait_apart(dve, dve_passed, stats_ready, 2 * value - 1)
                for i in range(QT):
                    last = nc.vector.bn_aggr(mom[:, i, :], bn[:, i, :])
                last.then_inc(stats_ready, 1)
                dve.wait_ge(chain_done, 2 * value)
                for i in range(QT):
                    last = nc.vector.tensor_scalar(dst[:, i, :], src[:, i, :], mom[:, i, 0:1], rstd[:, i:i + 1],
                                                   ALU.subtract, ALU.mult)
                last.then_inc(done, 1)

            def before(b):
                dve.wait_ge(x_loaded, 16 * b + 16)
                normalise(xn, x_in, 2 * b + 1, xn_ready)

            def head(b, h, n):
                for qt in range(QT):
                    m = QT * n + qt
                    k = STEPS * m
                    dve.wait_ge(scored, m + 1)
                    nc.vector.tensor_scalar(probs[:, :], score_ps[:, :], SCALE, None, ALU.mult)\
                      .then_inc(softmax_steps, 1)
                    dve.wait_ge(softmax_steps, k + 1)
                    nc.vector.tensor_scalar(probs[:, :], probs[:, :], -CLAMP, CLAMP, ALU.max, ALU.min)\
                      .then_inc(softmax_steps, 1)
                    dve.wait_ge(softmax_steps, k + 2)
                    nc.vector.tensor_tensor(probs[:, :], probs[:, :],
                                            true_decay[:, SEQ - P - P * qt:2 * SEQ - P - P * qt], ALU.mult)\
                      .then_inc(softmax_steps, 1)
                    dve.wait_ge(softmax_steps, k + 3)
                    nc.vector.reduce_max(top[:, :], probs[:, :], AX.X).then_inc(softmax_steps, 1)
                    dve.wait_ge(softmax_steps, k + 4)
                    nc.vector.tensor_tensor(probs[:, :], probs[:, :], top[:, :].to_broadcast([P, SEQ]),
                                            ALU.subtract).then_inc(softmax_steps, 1)
                    dve.wait_ge(exped, m + 1)
                    nc.vector.reduce_sum(total[:, :], probs[:, :], AX.X).then_inc(softmax_steps, 1)
                    dve.wait_ge(softmax_steps, k + 6)
                    nc.vector.reciprocal(share[:, :], total[:, :]).then_inc(softmax_steps, 1)
                    dve.wait_ge(softmax_steps, k + 7)
                    nc.vector.tensor_tensor(probs[:, :], probs[:, :], share[:, :].to_broadcast([P, SEQ]), ALU.mult)\
                      .then_inc(softmax_steps, 1)

            def after(b):
                dve.wait_ge(y_taken, b + 1)
                normalise(o, y, 2 * b + 2, y_normed)
                dve.wait_ge(y_normed, b + 1)
                nc.vector.tensor_tensor(y[:, :, :], o[:, :, :], x_in[:, :, :], ALU.add).then_inc(y_ready, 1)

            each_batch(dve, before, head, after)

        @block.gpsimd
        def _(pool):
            for used in sems.values():
                pool.sem_clear(used)
            nc.gpsimd.memset(half[:, :], -0.5).then_inc(half_ready, 1)
            wait_apart(pool, pool_passed, half_ready, 1)

            def deviation(value):
                wait_apart(pool, pool_passed, stats_ready, 2 * value)
                nc.gpsimd.tensor_scalar(small[:, :], mom[:, :, 1], LN_EPS, None, ALU.add).then_inc(chain_done, 1)
                wait_apart(pool, pool_passed, chain_done, 2 * value - 1)
                nc.gpsimd.tensor_tensor(rstd[:, :], small[:, :], half[:, :], ALU.pow).then_inc(chain_done, 1)

            each_batch(pool, lambda b: deviation(2 * b + 1), None, lambda b: deviation(2 * b + 2))


def sandwich_kernel(nc, t):
    t["scratch"] = nc.dram_tensor("split_terms", (2, 4, HEADS, HD, TERMS, SEQ), BF16, kind="Internal").ap()
    for name in ("x1", "ln_x1", "h"):
        t[name] = nc.dram_tensor(f"kept_{name}", (BATCH, SEQ, D), F32, kind="Internal").ap()
    for name, shape in (("kept_q", (D, SEQ)), ("kept_k", (D, SEQ)), ("kept_v", (SEQ, D)), ("kept_o", (SEQ, D))):
        t[name] = nc.dram_tensor(name, shape, F32, kind="Internal").ap()
    with nc.sbuf_tensor("scores_bounded", [1, 1], I32) as bounded:
        sems = {}
        attention_program(nc, t, BATCH, sems, bounded)
        flag = nc.values_load(bounded[0:1, 0:1], skip_runtime_bounds_check_because="a comparison made it, 0 or 1")
        with nc.If(flag < 1):
            clipped_attention_program(nc, t, sems)
            attention_program(nc, t, 0, sems)
        experts_program(nc, t)


_NAMES = {"L0_attn_x": "x", "L0_attn_Wq": "Wq", "L0_attn_Wk": "Wk", "L0_attn_Wv": "Wv", "L0_attn_Wo": "Wo",
          "L0_attn_W_down_kv": "Down", "L0_attn_W_up_k": "Up_k", "L0_attn_W_up_v": "Up_v",
          "L0_ffn_wq": "wq", "L0_ffn_wk": "wk", "L0_ffn_wv": "wv", "L0_ffn_wo": "wo",
          "L0_ffn_w_router": "w_router", "L0_ffn_wg": "wg", "L0_ffn_wu": "wu", "L0_ffn_wd": "wd",
          "L0_ffn_g1": "g1", "L0_ffn_g2": "g2"}


def tables():
    i = np.arange(SEQ, dtype=np.float64)
    off = np.arange(P)[:, None] - (np.arange(2 * SEQ - P)[None, :] - (SEQ - P))
    decay = np.exp(-DECAY * np.abs(off) - DECAY * off)
    inv = 1.0 / 10000.0 ** (np.arange(0, HD, 2, dtype=np.float32) / HD)
    freqs = np.einsum("i,j->ij", np.arange(SEQ, dtype=np.float32), inv.astype(np.float32))
    emb = np.concatenate([freqs, freqs], axis=-1)
    rows = np.arange(P)
    causal = np.zeros((P, SEQ), np.float32)
    causal[:, SEQ - P:] = np.where(rows[None, :] > rows[:, None], NEG, 0.0)
    n = np.arange(EXPERTS)
    made = {
        "ident": np.eye(P), "decay": decay,
        "grow": np.broadcast_to(np.exp(DECAY * i), (P, SEQ)), "shrink": np.broadcast_to(np.exp(-DECAY * i), (P, SEQ)),
        "cosines": np.tile(np.cos(emb).T, (HEADS, 1)), "sines": np.tile(np.sin(emb).T, (HEADS, 1)),
        "causal": causal, "true_decay": np.exp(-DECAY * np.abs(off)), "lower": np.broadcast_to((n[None, :] < n[:, None]), (P, EXPERTS, EXPERTS)),
    }
    return {k: np.ascontiguousarray(v, dtype=np.float32) for k, v in made.items()}


def kernel(**inputs):
    import concourse.bacc as bacc
    from concourse.bass_utils import run_bass_kernel_spmd

    nc = bacc.Bacc("TRN2", target_bir_lowering=False, num_devices=1)
    arrays, t = {}, {}
    named = {short: np.ascontiguousarray(inputs[name]) for name, short in _NAMES.items()}
    for name, a in {**named, **tables()}.items():
        arrays[f"in_{name}"] = a
        t[name] = nc.dram_tensor(f"in_{name}", a.shape, mybir.dt.from_np(a.dtype), kind="ExternalInput").ap()
    t["out"] = nc.dram_tensor("out_0", (BATCH, SEQ, D), F32, kind="ExternalOutput").ap()
    sandwich_kernel(nc, t)
    r = run_bass_kernel_spmd(nc, [arrays], core_ids=[0])
    return r.results[0]["out_0"]
```
